# Optimizing a Trainium2 kernel written in Bass

```python
import numpy as np
import jax
import jax.numpy as jnp

def _softmax(x, axis=-1):
    return jax.nn.softmax(x, axis=axis)
def _gelu(x):
    return jax.nn.gelu(x, approximate=True)
def _silu(x):
    return jax.nn.silu(x)
def _sigmoid(x):
    return jax.nn.sigmoid(x)
def _layernorm(x, axis=-1, eps=1e-5):
    m = jnp.mean(x, axis=axis, keepdims=True)
    v = jnp.var(x, axis=axis, keepdims=True)
    return (x - m) / jnp.sqrt(v + eps)
def _scatter_add(tgt, idx, src, axis=0):
    return tgt.at[idx].add(src)
def _segment_sum(src, seg, n):
    return jax.ops.segment_sum(src, seg, n)

kernel_name = 'mk_conv_seq_d4_conv_nchw256_d85dd5'

def setup_inputs(seed: int = 0):
    np.random.seed(seed)
    _w = jnp.asarray
    def _rec_inputs():
        import jax
        import jax.numpy as jnp
        _gk = jax.random.key(seed)
        x = -0.000929 + 1 * jax.random.normal(jax.random.fold_in(_gk, 1), (1, 256, 64, 64), jnp.float32)
        return x
    x = _rec_inputs()
    def _L0_conv_setup():
        import jax, jax.numpy as jnp
        import numpy as np
        NUM_HEADS = 8
        HEAD_DIM = 32

        def conv1x1(w, x):
            return jnp.einsum('oc,bchw->bohw', w, x)
        key = jax.random.key(seed)
        ks = jax.random.split(key, 6)
        C = 256
        x = jax.random.normal(ks[0], (1, C, 64, 64), dtype=jnp.float32)
        s = 1.0 / np.sqrt(C)
        Wf = jax.random.normal(ks[1], (C, C), dtype=jnp.float32) * s
        Wg = jax.random.normal(ks[2], (C, C), dtype=jnp.float32) * s
        Wh = jax.random.normal(ks[3], (C, C), dtype=jnp.float32) * s
        Wv = jax.random.normal(ks[4], (C, C), dtype=jnp.float32) * s
        Wm = jax.random.normal(ks[5], (C, C), dtype=jnp.float32) * s
        return {'x': x, 'Wf': Wf, 'Wg': Wg, 'Wh': Wh, 'Wv': Wv, 'Wm': Wm}
    _L0_conv_all = _L0_conv_setup()
    _L0_conv_in = {k: v for k, v in _L0_conv_all.items() if k in ('Wf', 'Wg', 'Wh', 'Wv', 'Wm', )}
    del _L0_conv_all

    def _L1_conv_setup():
        import jax, jax.numpy as jnp
        import numpy as np
        B, C, H, W = (8, 256, 64, 64)
        CQK = C // 8
        key = jax.random.key(seed)
        ks = jax.random.split(key, 8)
        s = 0.05
        return {'x': jax.random.normal(ks[0], (B, C, H, W), dtype=jnp.float32), 'wq': jax.random.normal(ks[1], (CQK, C), dtype=jnp.float32) * s, 'bq': jax.random.normal(ks[2], (CQK,), dtype=jnp.float32) * s, 'wk': jax.random.normal(ks[3], (CQK, C), dtype=jnp.float32) * s, 'bk': jax.random.normal(ks[4], (CQK,), dtype=jnp.float32) * s, 'wv': jax.random.normal(ks[5], (C, C), dtype=jnp.float32) * s, 'bv': jax.random.normal(ks[6], (C,), dtype=jnp.float32) * s, 'gamma': jax.random.normal(ks[7], (1,), dtype=jnp.float32)}
    _L1_conv_all = _L1_conv_setup()
    _L1_conv_in = {k: v for k, v in _L1_conv_all.items() if k in ('wq', 'bq', 'wk', 'bk', 'wv', 'bv', 'gamma', )}
    del _L1_conv_all

    def _L2_conv_setup():
        import jax, jax.numpy as jnp
        import numpy as np
        C = 256
        NUM_HEADS = 4
        HEAD_DIM = C // NUM_HEADS

        def _proj(x, Wmat, b):
            return jnp.einsum('nchw,oc->nohw', x, Wmat) + b[None, :, None, None]
        key = jax.random.key(seed)
        ks = jax.random.split(key, 9)
        N, H, W = (4, 48, 48)
        s = 1.0 / np.sqrt(C)
        return {'x': jax.random.normal(ks[0], (N, C, H, W), dtype=jnp.float32), 'Wq': jax.random.normal(ks[1], (C, C), dtype=jnp.float32) * s, 'bq': jax.random.normal(ks[2], (C,), dtype=jnp.float32) * 0.01, 'Wk': jax.random.normal(ks[3], (C, C), dtype=jnp.float32) * s, 'bk': jax.random.normal(ks[4], (C,), dtype=jnp.float32) * 0.01, 'Wv': jax.random.normal(ks[5], (C, C), dtype=jnp.float32) * s, 'bv': jax.random.normal(ks[6], (C,), dtype=jnp.float32) * 0.01, 'Wo': jax.random.normal(ks[7], (C, C), dtype=jnp.float32) * s, 'bo': jax.random.normal(ks[8], (C,), dtype=jnp.float32) * 0.01}
    _L2_conv_all = _L2_conv_setup()
    _L2_conv_in = {k: v for k, v in _L2_conv_all.items() if k in ('Wq', 'bq', 'Wk', 'bk', 'Wv', 'bv', 'Wo', 'bo', )}
    del _L2_conv_all

    def _L3_conv_setup():
        import jax, jax.numpy as jnp
        import numpy as np
        C_IN = 256
        C_INT = C_IN // 2

        def _conv1x1(x, w, b):
            return jnp.einsum('bchw,oc->bohw', x, w) + b[None, :, None, None]
        key = jax.random.key(seed)
        ks = jax.random.split(key, 9)
        B, H, W = (8, 64, 64)
        s_in = 1.0 / np.sqrt(C_IN)
        s_int = 1.0 / np.sqrt(C_INT)
        return {'x': jax.random.normal(ks[0], (B, C_IN, H, W), dtype=jnp.float32), 'g_w': jax.random.normal(ks[1], (C_INT, C_IN), dtype=jnp.float32) * s_in, 'g_b': jax.random.normal(ks[2], (C_INT,), dtype=jnp.float32) * s_in, 'theta_w': jax.random.normal(ks[3], (C_INT, C_IN), dtype=jnp.float32) * s_in, 'theta_b': jax.random.normal(ks[4], (C_INT,), dtype=jnp.float32) * s_in, 'phi_w': jax.random.normal(ks[5], (C_INT, C_IN), dtype=jnp.float32) * s_in, 'phi_b': jax.random.normal(ks[6], (C_INT,), dtype=jnp.float32) * s_in, 'W_w': jax.random.normal(ks[7], (C_IN, C_INT), dtype=jnp.float32) * s_int, 'W_b': jax.random.normal(ks[8], (C_IN,), dtype=jnp.float32) * s_int}
    _L3_conv_all = _L3_conv_setup()
    _L3_conv_in = {k: v for k, v in _L3_conv_all.items() if k in ('g_w', 'g_b', 'theta_w', 'theta_b', 'phi_w', 'phi_b', 'W_w', 'W_b', )}
    del _L3_conv_all

    return {
        "x": x,
        "L0_conv_Wf": _L0_conv_in["Wf"],
        "L0_conv_Wg": _L0_conv_in["Wg"],
        "L0_conv_Wh": _L0_conv_in["Wh"],
        "L0_conv_Wv": _L0_conv_in["Wv"],
        "L0_conv_Wm": _L0_conv_in["Wm"],
        "L1_conv_wq": _L1_conv_in["wq"],
        "L1_conv_bq": _L1_conv_in["bq"],
        "L1_conv_wk": _L1_conv_in["wk"],
        "L1_conv_bk": _L1_conv_in["bk"],
        "L1_conv_wv": _L1_conv_in["wv"],
        "L1_conv_bv": _L1_conv_in["bv"],
        "L1_conv_gamma": _L1_conv_in["gamma"],
        "L2_conv_Wq": _L2_conv_in["Wq"],
        "L2_conv_bq": _L2_conv_in["bq"],
        "L2_conv_Wk": _L2_conv_in["Wk"],
        "L2_conv_bk": _L2_conv_in["bk"],
        "L2_conv_Wv": _L2_conv_in["Wv"],
        "L2_conv_bv": _L2_conv_in["bv"],
        "L2_conv_Wo": _L2_conv_in["Wo"],
        "L2_conv_bo": _L2_conv_in["bo"],
        "L3_conv_g_w": _L3_conv_in["g_w"],
        "L3_conv_g_b": _L3_conv_in["g_b"],
        "L3_conv_theta_w": _L3_conv_in["theta_w"],
        "L3_conv_theta_b": _L3_conv_in["theta_b"],
        "L3_conv_phi_w": _L3_conv_in["phi_w"],
        "L3_conv_phi_b": _L3_conv_in["phi_b"],
        "L3_conv_W_w": _L3_conv_in["W_w"],
        "L3_conv_W_b": _L3_conv_in["W_b"],
    }

def reference(x, L0_conv_Wf, L0_conv_Wg, L0_conv_Wh, L0_conv_Wv, L0_conv_Wm, L1_conv_wq, L1_conv_bq, L1_conv_wk, L1_conv_bk, L1_conv_wv, L1_conv_bv, L1_conv_gamma, L2_conv_Wq, L2_conv_bq, L2_conv_Wk, L2_conv_bk, L2_conv_Wv, L2_conv_bv, L2_conv_Wo, L2_conv_bo, L3_conv_g_w, L3_conv_g_b, L3_conv_theta_w, L3_conv_theta_b, L3_conv_phi_w, L3_conv_phi_b, L3_conv_W_w, L3_conv_W_b):
    import jax
    import jax.numpy as jnp
    def _L0_conv_ref(x, Wf, Wg, Wh, Wv, Wm):
        import jax, jax.numpy as jnp
        import numpy as np
        NUM_HEADS = 8
        HEAD_DIM = 32

        def conv1x1(w, x):
            return jnp.einsum('oc,bchw->bohw', w, x)
        B, C, H, W = x.shape
        Q = conv1x1(Wf, x).reshape(B, -1, NUM_HEADS, HEAD_DIM)
        K = conv1x1(Wg, x).reshape(B, -1, NUM_HEADS, HEAD_DIM)
        V = conv1x1(Wh, x).reshape(B, -1, NUM_HEADS, HEAD_DIM)
        softmax_temp = 1.0 / jnp.sqrt(jnp.asarray(HEAD_DIM, x.dtype))
        QK = jnp.einsum('nlhd,nshd->nlsh', Q, K)
        A = jax.nn.softmax(softmax_temp * QK, axis=2)
        z = jnp.einsum('nlsh,nshd->nlhd', A, V)
        z = z.reshape(B, -1, NUM_HEADS * HEAD_DIM) @ Wm.T
        z = jnp.transpose(z, (0, 2, 1)).reshape(B, C, H, W)
        z = conv1x1(Wv, z)
        return z + x

    def _L1_conv_ref(x, wq, bq, wk, bk, wv, bv, gamma):
        import jax, jax.numpy as jnp
        import numpy as np
        B, C, H, W = (8, 256, 64, 64)
        CQK = C // 8
        b, c, h, w = x.shape
        xf = x.reshape(b, c, h * w)
        f = jnp.einsum('oc,bcn->bon', wq, xf) + bq[None, :, None]
        g = jnp.einsum('oc,bcn->bon', wk, xf) + bk[None, :, None]
        hh = jnp.einsum('oc,bcn->bon', wv, xf) + bv[None, :, None]
        scores = jnp.einsum('boi,boj->bij', f, g)
        beta = jax.nn.softmax(scores, axis=1)
        o = gamma[0] * jnp.einsum('bci,bij->bcj', hh, beta) + xf
        return o.reshape(b, c, h, w)

    def _L2_conv_ref(x, Wq, bq, Wk, bk, Wv, bv, Wo, bo):
        import jax, jax.numpy as jnp
        import numpy as np
        C = 256
        NUM_HEADS = 4
        HEAD_DIM = C // NUM_HEADS

        def _proj(x, Wmat, b):
            return jnp.einsum('nchw,oc->nohw', x, Wmat) + b[None, :, None, None]
        N, Cin, H, W = x.shape
        S = H * W

        def heads(t):
            return t.reshape(N, NUM_HEADS, HEAD_DIM, S).transpose(0, 1, 3, 2)
        q = heads(_proj(x, Wq, bq))
        k = heads(_proj(x, Wk, bk))
        v = heads(_proj(x, Wv, bv))
        scale = 1.0 / np.sqrt(HEAD_DIM).astype(np.float32)
        scores = jnp.einsum('nhsd,nhtd->nhst', q, k) * scale
        attn = jax.nn.softmax(scores, axis=-1)
        out = jnp.einsum('nhst,nhtd->nhsd', attn, v)
        out = out.transpose(0, 1, 3, 2).reshape(N, Cin, H, W)
        out = _proj(out, Wo, bo)
        return x + out

    def _L3_conv_ref(x, g_w, g_b, theta_w, theta_b, phi_w, phi_b, W_w, W_b):
        import jax, jax.numpy as jnp
        import numpy as np
        C_IN = 256
        C_INT = C_IN // 2

        def _conv1x1(x, w, b):
            return jnp.einsum('bchw,oc->bohw', x, w) + b[None, :, None, None]
        B, C, H, W = x.shape
        N = H * W
        g_x = _conv1x1(x, g_w, g_b).reshape(B, C_INT, N)
        theta_x = _conv1x1(x, theta_w, theta_b).reshape(B, C_INT, N)
        phi_x = _conv1x1(x, phi_w, phi_b).reshape(B, C_INT, N)
        f = jnp.einsum('bci,bcj->bij', theta_x, phi_x)
        f_div_C = jax.nn.softmax(f, axis=-1)
        y = jnp.einsum('bij,bcj->bci', f_div_C, g_x)
        y = y.reshape(B, C_INT, H, W)
        y = _conv1x1(y, W_w, W_b)
        return x + y

    def _gn(v, G=32, eps=1e-5):
        B_, C_, H_, W_ = v.shape
        g = v.reshape(B_, G, C_ // G, H_, W_)
        m = jnp.mean(g, axis=(2, 3, 4), keepdims=True)
        s = jnp.var(g, axis=(2, 3, 4), keepdims=True)
        return ((g - m) / jnp.sqrt(s + eps)).reshape(v.shape)

    def _ln_c(v, eps=1e-6):
        m = jnp.mean(v, axis=1, keepdims=True)
        s = jnp.var(v, axis=1, keepdims=True)
        return (v - m) / jnp.sqrt(s + eps)

    def _ln_t(v, eps=1e-5):
        m = jnp.mean(v, axis=-1, keepdims=True)
        s = jnp.var(v, axis=-1, keepdims=True)
        return (v - m) / jnp.sqrt(s + eps)

    def _to_tokens(v):
        B_, C_, H_, W_ = v.shape
        return v.reshape(B_, C_, H_ * W_).transpose(0, 2, 1)
    def _from_tokens(t, like):
        B_, C_, H_, W_ = like.shape
        return t.transpose(0, 2, 1).reshape(B_, C_, H_, W_)

    x = _L0_conv_ref(x, L0_conv_Wf, L0_conv_Wg, L0_conv_Wh, L0_conv_Wv, L0_conv_Wm)
    x = _L1_conv_ref(x, L1_conv_wq, L1_conv_bq, L1_conv_wk, L1_conv_bk, L1_conv_wv, L1_conv_bv, L1_conv_gamma)
    x = _L2_conv_ref(x, L2_conv_Wq, L2_conv_bq, L2_conv_Wk, L2_conv_bk, L2_conv_Wv, L2_conv_bv, L2_conv_Wo, L2_conv_bo)
    x = _L3_conv_ref(x, L3_conv_g_w, L3_conv_g_b, L3_conv_theta_w, L3_conv_theta_b, L3_conv_phi_w, L3_conv_phi_b, L3_conv_W_w, L3_conv_W_b)
    return x


_drawn_inputs = setup_inputs


def setup_inputs(seed=0):
    import zlib

    import numpy as np

    out = dict(_drawn_inputs(seed))
    spreads = {}
    factors = {'L1_conv_bq': 64.0,
     'L1_conv_bk': 5.755,
     'L1_conv_bv': 5.31,
     'L2_conv_bq': 26.557,
     'L2_conv_bk': 64.0,
     'L3_conv_phi_b': 64.0}
    for name, (base, spread) in spreads.items():
        noise = np.random.default_rng([zlib.crc32(name.encode()), seed]).standard_normal(out[name].shape)
        drawn = base * np.exp(spread * noise) if base else spread * noise
        out[name] = jnp.asarray(drawn.astype(out[name].dtype))
    for name, factor in factors.items():
        out[name] = (out[name] * factor).astype(out[name].dtype)
    return out
```

```python
import concourse.bass as bass
from concourse import mybir
from contextlib import ExitStack

F32 = mybir.dt.float32
F32R = mybir.dt.float32r
ALU = mybir.AluOpType
ACT = mybir.ActivationFunctionType
AX = mybir.AxisListType

C, T, P = 256, 4096, 128
CH = C // P
LB = 512
NB = T // LB
NC = T // P
GRID = 16
RING = 8

STACK32 = dict(q_parts=((0, 0, 0), (0, 32, 1), (0, 64, 0)), k_parts=((0, 0, 0), (0, 32, 0), (0, 64, 1)),
               products=((0, 0, 96),), shift=(0, 96), shift_product=0, k_slots=1, q_slots=1)
STACK64 = dict(q_parts=((0, 0, 0), (0, 64, 1), (1, 0, 0)), k_parts=((0, 0, 0), (0, 64, 0), (1, 0, 1)),
               products=((0, 0, 128), (1, 1, 64)), shift=(1, 64), shift_product=1, k_slots=2, q_slots=2)
STACK128 = dict(q_parts=((0, 0, 0), (1, 0, 1)), k_parts=((0, 0, 0), (1, 0, 1)),
                products=((0, 0, 128), (0, 1, 128), (1, 0, 128)), shift=(2, 0), shift_product=None,
                k_slots=2, q_slots=2)
MOSTLY_POOL = tuple(c for c in range(NC) if c % 2 == 0 or c in (5, 15, 25))
EVEN = tuple(range(0, NC, 2))
LAYERS = (
    dict(heads=8, dq=32, dv=32, scale=32 ** -0.5, tile=1024, pool_chunks=MOSTLY_POOL, **STACK32),
    dict(heads=1, dq=32, dv=256, scale=1.0, tile=512, pool_chunks=EVEN, **STACK32),
    dict(heads=4, dq=64, dv=64, scale=64 ** -0.5, tile=1024, pool_chunks=EVEN, **STACK64),
    dict(heads=1, dq=128, dv=128, scale=1.0, tile=1024, pool_chunks=EVEN, **STACK128),
)

B_L1_QK, B_L1_V, B_GAMMA, B_L2_Q, B_L2_K, B_L2_V, B_L2_O = 0, 1, 3, 4, 6, 8, 10
B_L3_Q, B_L3_K, B_L3_V, B_L3_O, B_ZERO, B_COLS = 12, 13, 14, 15, 17, 18
K_IDENT, K_ONES, K_SUM32, K_SUM64, K_COLS = 0, P, 2 * P, 2 * P + 32, 2 * P + 96


def wait_count(eng, sem, value):
    if isinstance(value, int) and value <= 0:
        return
    eng.wait_ge(sem, value)


class Memory:

    def __init__(self, nc, ctx):
        def sb(name, shape, dt=F32):
            return ctx.enter_context(nc.sbuf_tensor(name, shape, dt))

        self.x = sb("x", [P, CH, T])
        self.qk = sb("qk", [P, 27 * 1024], F32R)
        self.v = sb("v", [P, 8192])
        self.probs = sb("probs", [P, RING, LB])
        self.sums = sb("sums", [P, 2, LB])
        self.z = sb("z", [P, 2, LB])
        self.recip = sb("recip", [P, LB])
        self.bias = sb("bias", [P, B_COLS])
        self.const = sb("const", [P, K_COLS])
        self.rowmax = sb("rowmax", [P, 4, 8])
        self.negmax = sb("negmax", [P, 4])
        self.shift = sb("shift", [P, 4, 2])
        self.ones2 = sb("ones2", [2, P], F32R)
        self.psum = [ctx.enter_context(nc.psum_tensor(f"bank{i}", [P, 2, LB], F32)) for i in range(4)]

        def dram(name, shape, dt):
            return nc.dram_tensor(name, shape, dt, kind="Internal").ap()

        self.q_dram = dram("q_dram", (2, C, T), F32)
        self.k_dram = dram("k_dram", (2, C, T), F32)
        self.v_dram = dram("v_dram", (T, C), F32)
        self.z_dram = dram("z_dram", (C, T), F32)

    def bank(self, i):
        return self.psum[i // 2][:, i % 2, :]


def load_phase(nc, sem, m, x, bias, const):
    loaded = sem("inputs_loaded")
    with nc.Block() as block:
        @block.sync
        def _(sp):
            for half in range(CH):
                sp.dma_start(m.x[:, half, :], x[half * P:(half + 1) * P, :]).then_inc(loaded, 16)
            sp.dma_start(m.bias[:, :], bias).then_inc(loaded, 16)
            sp.dma_start(m.const[:, :], const).then_inc(loaded, 16)
            sp.wait_ge(loaded, 64)


def weights_view(m, cols):
    return m.probs[:, :, :].rearrange("p a b -> p (a b)")[:, 0:CH * cols].rearrange("p (k n) -> p k n", k=CH)


def passes(eng, trips, body):
    body(0)
    if trips > 1:
        with eng.Fori(1, trips) as trip:
            body(trip)


def project_phase(nc, sem, m, layer, w):
    cfg = LAYERS[layer]
    cols = w.shape[1]
    wt = weights_view(m, cols)
    hi = [m.qk[:, s * LB:(s + 1) * LB] for s in range(4)]
    lo = [m.qk[:, (4 + s) * LB:(5 + s) * LB] for s in range(4)]
    vs = [m.v[:, s * LB:(s + 1) * LB] for s in range(4)]
    w_loaded = sem(f"w_loaded{layer}")
    qk_done, hi_done, lo_done = sem(f"qk_done{layer}"), sem(f"hi_done{layer}"), sem(f"lo_done{layer}")
    v_done, v_copied = sem(f"v_done{layer}"), sem(f"v_copied{layer}")
    qk_stored = [sem(f"qk_stored{layer}_{s}") for s in range(4)]
    v_stored = [sem(f"v_stored{layer}_{s}") for s in range(4)]

    groups, rows = ((2, P), (1, 64), (4, P), (2, P))[layer]
    trips, body = ((1, 32), (2, 4), (4, 8), (4, 4))[layer]
    trip_px = body // groups * LB
    stores = (4, 4, 2, 2)[layer]
    v_trips, v_body = (4, 4) if layer == 0 else (1, NC)
    v_col = (2 * C, 64, 2 * C, C)[layer]
    v_n = LB if layer == 0 else cfg["heads"] * cfg["dv"]

    def bias_of(i):
        col = (B_ZERO, B_L1_QK, B_L2_Q + i % groups, B_L3_Q + i % groups)[layer]
        return m.bias[0:rows, col:col + 1]

    with nc.Block() as block:
        @block.tensor
        def _(pe):
            pe.wait_ge(w_loaded, 16 * CH)

            def qk_tiles(trip):
                for i in range(body):
                    wait_count(pe, lo_done, trip * body + i - 3)
                    for k in range(CH):
                        if layer == 0:
                            lhs, rhs = m.x[:, k, i * P:(i + 1) * P], wt[:, k, 0:LB]
                        else:
                            lhs = wt[:, k, i % groups * rows:(i % groups + 1) * rows]
                            rhs = m.x[:, k, bass.ds(trip * trip_px + i // groups * LB, LB)]
                        mm = nc.tensor.matmul(m.bank(i % 4)[0:rows, :], lhs, rhs, start=k == 0, stop=k == CH - 1)
                    mm.then_inc(qk_done, 1)

            def v_tiles(trip):
                for i in range(v_body):
                    wait_count(pe, v_copied, trip * v_body + i - 3)
                    for k in range(CH):
                        if layer == 0:
                            lhs = wt[:, k, v_col + i % CH * P:v_col + (i % CH + 1) * P]
                            rhs = m.x[:, k, bass.ds(trip * (2 * LB) + i // CH * LB, LB)]
                        else:
                            lhs, rhs = m.x[:, k, i * P:(i + 1) * P], wt[:, k, v_col:v_col + v_n]
                        mm = nc.tensor.matmul(m.bank(4 + i % 4)[:, 0:v_n], lhs, rhs, start=k == 0, stop=k == CH - 1)
                    mm.then_inc(v_done, 1)

            passes(pe, trips, qk_tiles)
            passes(pe, v_trips, v_tiles)

        @block.scalar
        def _(act):
            def round_hi(trip):
                for i in range(body):
                    act.wait_ge(qk_done, trip * body + i + 1)
                    wait_count(act, qk_stored[i % 4], (trip * (body // 4) + i // 4) * (16 * stores))
                    nc.scalar.activation(hi[i % 4][0:rows, :], m.bank(i % 4)[0:rows, :], ACT.Identity,
                                         bias=bias_of(i)).then_inc(hi_done, 1)

            passes(act, trips, round_hi)

        @block.vector
        def _(dve):
            def round_lo(trip):
                for i in range(body):
                    dve.wait_ge(hi_done, trip * body + i + 1)
                    nc.vector.scalar_tensor_tensor(out=lo[i % 4][0:rows, :], in0=m.bank(i % 4)[0:rows, :],
                                                   scalar=bias_of(i), in1=hi[i % 4][0:rows, :],
                                                   op0=ALU.add, op1=ALU.subtract).then_inc(lo_done, 1)

            def copy_v(trip):
                for i in range(v_body):
                    dve.wait_ge(v_done, trip * v_body + i + 1)
                    wait_count(dve, v_stored[i % 4], (trip * (v_body // 4) + i // 4) * 16)
                    nc.vector.tensor_copy(vs[i % 4][:, 0:v_n], m.bank(4 + i % 4)[:, 0:v_n]).then_inc(v_copied, 1)

            passes(dve, trips, round_lo)
            passes(dve, v_trips, copy_v)

        @block.sync
        def _(sp):
            for k in range(CH):
                sp.dma_start(wt[:, k, :], w[k * P:(k + 1) * P, :]).then_inc(w_loaded, 16)

            def store_qk(trip):
                for i in range(body):
                    sp.wait_ge(lo_done, trip * body + i + 1)
                    for part, tile in enumerate((hi[i % 4], lo[i % 4])):
                        if layer == 0:
                            at = (slice(i % 2 * P, (i % 2 + 1) * P), slice(i // 2 * C, (i // 2 + 1) * C))
                            moves = ((m.q_dram[part][at], tile[:, 0:C]), (m.k_dram[part][at], tile[:, C:2 * C]))
                        else:
                            px = bass.ds(trip * trip_px + i // groups * LB, LB)
                            if layer == 1:
                                moves = ((m.q_dram[part, 0:32, px], tile[0:32, :]), (m.k_dram[part, 0:32, px], tile[32:64, :]))
                            else:
                                g = i % groups
                                half = g % (groups // 2) * P
                                to = m.q_dram if g < groups // 2 else m.k_dram
                                moves = ((to[part, half:half + P, px], tile[:, :]),)
                        for dst, src in moves:
                            sp.dma_start(dst, src.bitcast(F32)).then_inc(qk_stored[i % 4], 16)

            v_tokens = m.v_dram.rearrange("(j h p) n -> h p j n", h=CH, p=P)

            def store_v(trip):
                for i in range(v_body):
                    sp.wait_ge(v_copied, trip * v_body + i + 1)
                    if layer == 0:
                        dst = v_tokens[i % CH][:, bass.ds(trip * 4 + i // CH * 2, 2), :]
                        src = vs[i % 4].rearrange("p (j n) -> p j n", j=2)
                    else:
                        dst, src = m.v_dram[i * P:(i + 1) * P, 0:v_n], vs[i % 4][:, 0:v_n]
                    sp.dma_start(dst, src).then_inc(v_stored[i % 4], 16)

            passes(sp, trips, store_qk)
            passes(sp, v_trips, store_v)
            for s in range(4):
                sp.wait_ge(qk_stored[s], trips * (body // 4) * 16 * stores)
                sp.wait_ge(v_stored[s], v_trips * (v_body // 4) * 16)


def attention_phase(nc, sem, m, layer):
    cfg = LAYERS[layer]
    H, dq, dv, products = cfg["heads"], cfg["dq"], cfg["dv"], cfg["products"]
    ks, qs, tile = cfg["k_slots"], cfg["q_slots"], cfg["tile"]
    U = H * NB
    NT, per_row = 4 * T // tile, T // tile
    accs = -(-dv // P)
    width = min(dv, P)
    col_tiles = P // width
    shift_slot, shift_row = cfg["shift"]
    b_slots = max(qs, shift_slot + 1)
    n_q, n_k = len(cfg["q_parts"]), len(cfg["k_parts"])
    pool_chunks = cfg["pool_chunks"]
    vec_chunks = tuple(c for c in range(NC) if c not in pool_chunks)
    n_pool, n_vec = len(pool_chunks) - 1, len(vec_chunks) - 1
    tiles_at = [[k for k in range(NT) if k * 28 // NT == c] for c in range(NC)]
    vec_at = [[j for j in range(n_vec) if min(vec_chunks[j + 1] + 2, NC - 1) == c] for c in range(NC)]

    at = 0

    def take(n):
        nonlocal at
        at += n
        return m.qk[:, at - n:at]

    k_still = take(ks * T).rearrange("p (s n) -> p s n", s=ks)
    k_move = take(2 * ks * T) if H > 1 else None
    q_still = take(qs * LB).rearrange("p (s n) -> p s n", s=qs)
    q_move = take(2 * b_slots * LB)
    v_head = m.v[:, 0:NC * dv].rearrange("p (c d) -> p c d", c=NC)
    rounded = m.shift[:, :, :].bitcast(F32R)

    def moving_q(u, slot, r0, r1):
        return q_move[r0:r1, bass.ds(u % 2 * (b_slots * LB) + slot * LB, LB)]

    def moving_k(b, slot, rows, col):
        if H == 1:
            return k_still[0:rows, slot, col:col + LB]
        return k_move[0:rows, bass.ds(b // NB % 2 * (ks * T) + slot * T + col, LB)]

    def max_bank(k):
        return m.psum[k % 2][:, :, :] if tile == 2 * LB else m.psum[0][:, k % 2:k % 2 + 1, :]

    fin = m.bank(7)
    acc = [m.bank(6), m.bank(3)][0:accs]

    s = {n: sem(f"{n}{layer}") for n in (
        "ones_ready", "max_ready", "max_taken", "max_chained", "shift_ready", "shift_moved", "shift_copied",
        "scores_ready", "probs_ready", "values_done", "values_copied", "pool_summed", "vec_summed",
        "den_ready", "values_folded", "recip_ready", "z_ready", "z_stored", "k_moving_in", "q_moving_in")}
    q_still_in = [sem(f"q_still_in{layer}_{t}") for t in range(4)]
    k_still_in = [sem(f"k_still_in{layer}_{t}") for t in range(4)]
    v_in = [sem(f"v_in{layer}_{t}") for t in range(4)]

    def units(eng, unit):
        unit(0, True, False)
        with eng.Fori(1, U - 1) as u:
            unit(u, False, False)
        unit(U - 1, False, True)

    with nc.Block() as block:
        @block.tensor
        def _(pe):
            def max_tile(b, k):
                t, part = k // per_row, k % per_row
                if k == 0:
                    if H > 1:
                        pe.wait_ge(s["k_moving_in"], (b // NB + 1) * (16 * n_k))
                    elif isinstance(b, int) and b == 0:
                        for piece in range(4):
                            pe.wait_ge(k_still_in[piece], 16 * n_k)
                if part == 0:
                    pe.wait_ge(q_still_in[t], (b + 1) * (16 * n_q))
                wait_count(pe, s["max_taken"], b * NT + k - 1)
                for n in range(tile // LB):
                    col = part * tile + n * LB
                    for i, (sk, sq, rows) in enumerate(products):
                        mm = nc.tensor.matmul(max_bank(k)[:, n, :], q_still[0:rows, sq, t * P:(t + 1) * P],
                                              moving_k(b, sk, rows, col), start=i == 0, stop=i == len(products) - 1)
                mm.then_inc(s["max_ready"], 1)

            def shift_rows(b):
                pe.wait_ge(s["shift_ready"], b + 1)
                wait_count(pe, s["z_ready"], b - 1)
                for t in range(4):
                    mm = nc.tensor.matmul(fin[0:2, t * P:(t + 1) * P], m.shift[:, t, :],
                                          m.const[:, K_IDENT:K_IDENT + P], start=True, stop=True)
                mm.then_inc(s["shift_moved"], 1)

            def scores(u, c):
                if c == 0:
                    pe.wait_ge(s["shift_copied"], u + 1)
                    pe.wait_ge(s["q_moving_in"], (u + 1) * (16 * n_q))
                if c % 8 == 0:
                    pe.wait_ge(k_still_in[c // 8], (u // NB + 1) * (16 * n_k))
                wait_count(pe, s["probs_ready"], u * NC + c - 1)
                out = m.bank(4 + c % 2)
                for i, (sk, sq, rows) in enumerate(products):
                    rows += 2 * (i == cfg["shift_product"])
                    last = i == len(products) - 1 and cfg["shift_product"] is not None
                    mm = nc.tensor.matmul(out, k_still[0:rows, sk, c * P:(c + 1) * P], moving_q(u, sq, 0, rows),
                                          start=i == 0, stop=last)
                if cfg["shift_product"] is None:
                    mm = nc.tensor.matmul(out, m.ones2[:, :], moving_q(u, shift_slot, 0, 2), start=False, stop=True)
                mm.then_inc(s["scores_ready"], 1)

            def values(u, g):
                pe.wait_ge(s["probs_ready"], u * NC + 4 * g + 4)
                if g == 0:
                    wait_count(pe, s["values_copied"], u)
                if g % 2 == 0:
                    pe.wait_ge(v_in[g // 2], (u // NB + 1) * 16)
                for c in range(4 * g, 4 * g + 4):
                    r = c % col_tiles * width
                    for a in range(accs):
                        mm = nc.tensor.matmul(acc[a][r:r + width, :], v_head[:, c, a * P:a * P + width],
                                              m.probs[:, c % RING, :], start=c < col_tiles, stop=c >= NC - col_tiles)
                mm.then_inc(s["values_done"], 1)

            def denominators(u):
                pe.wait_ge(s["pool_summed"], (u + 1) * n_pool)
                pe.wait_ge(s["vec_summed"], (u + 1) * n_vec)
                for e in range(2):
                    mm = nc.tensor.matmul(fin[0:width, :], m.const[:, K_ONES:K_ONES + width], m.sums[:, e, :],
                                          start=e == 0, stop=e == 1)
                mm.then_inc(s["den_ready"], 1)

            def fold_values(u):
                pe.wait_ge(s["values_copied"], u + 1)
                k = K_SUM32 if width == 32 else K_SUM64
                nc.tensor.matmul(fin[width:2 * width, :], m.const[:, k:k + width], m.z[:, 0, :],
                                 start=True, stop=True).then_inc(s["values_folded"], 1)

            def unit(u, first, last):
                for c in range(NC):
                    if not last:
                        for k in tiles_at[c]:
                            max_tile(u + 1, k)
                    scores(u, c)
                    if c % 4 == 3:
                        if c == 3 and not first:
                            denominators(u - 1)
                        if c == NC - 1 and not last:
                            shift_rows(u + 1)
                        if c > 3:
                            values(u, c // 4 - 1)
                        elif not first:
                            values(u - 1, NC // 4 - 1)
                    if c == 7 and not first and col_tiles > 1:
                        fold_values(u - 1)

            pe.wait_ge(s["ones_ready"], 1)
            for k in range(NT):
                max_tile(0, k)
            shift_rows(0)
            units(pe, unit)
            values(U - 1, NC // 4 - 1)
            denominators(U - 1)
            if col_tiles > 1:
                fold_values(U - 1)

        @block.scalar
        def _(act):
            def copy_shift(u):
                act.wait_ge(s["shift_moved"], u + 1)
                nc.scalar.activation(moving_q(u, shift_slot, shift_row, shift_row + 2), fin[0:2, :],
                                     ACT.Copy).then_inc(s["shift_copied"], 1)

            def free_probs(u, c):
                if c % 4 == 0:
                    wait_count(act, s["values_done"], u * (NC // 4) + c // 4 - 1)
                before = c - RING
                uu = u if before >= 0 else u - 1
                before %= NC
                chunks, n, name = ((pool_chunks, n_pool, "pool_summed") if before in pool_chunks
                                   else (vec_chunks, n_vec, "vec_summed"))
                wait_count(act, s[name], uu * n + max(chunks.index(before), 1))

            def copy_values(u):
                act.wait_ge(s["values_done"], (u + 1) * (NC // 4))
                wait_count(act, s["z_stored"], u * (16 * accs))
                for a in range(accs):
                    op = nc.scalar.activation(m.z[:, a, :], acc[a], ACT.Copy)
                op.then_inc(s["values_copied"], 1)

            def store_z(u):
                act.wait_ge(s["z_ready"], u + 1)
                for a in range(accs):
                    act.dma_start(m.z_dram[bass.ds(u // NB * dv + a * P, width), bass.ds(u % NB * LB, LB)],
                                  m.z[0:width, a, :]).then_inc(s["z_stored"], 16)

            def unit(u, first, last):
                for c in range(NC):
                    act.wait_ge(s["scores_ready"], u * NC + c + 1)
                    free_probs(u, c)
                    nc.scalar.activation(m.probs[:, c % RING, :], m.bank(4 + c % 2), ACT.Exp,
                                         scale=cfg["scale"]).then_inc(s["probs_ready"], 1)
                    if c == 5 and not first:
                        copy_values(u - 1)
                    if c == 24 and not first:
                        store_z(u - 1)
                if not last:
                    copy_shift(u + 1)

            copy_shift(0)
            units(act, unit)
            copy_values(U - 1)
            store_z(U - 1)
            act.wait_ge(s["z_stored"], U * 16 * accs)

        @block.vector
        def _(dve):
            def take_max(b, k):
                dve.wait_ge(s["max_ready"], b * NT + k + 1)
                if k == 0:
                    wait_count(dve, s["shift_ready"], b)
                src = max_bank(k).rearrange("p a n -> p (a n)")
                nc.vector.reduce_max(m.rowmax[:, k // per_row, k % per_row:k % per_row + 1], src,
                                     AX.X).then_inc(s["max_taken"], 1)

            def make_shift(b):
                dve.wait_ge(s["max_taken"], (b + 1) * NT)
                nc.vector.reduce_max(m.negmax[:, :], m.rowmax[:, :, 0:per_row], AX.X).then_inc(s["max_chained"], 1)
                dve.wait_ge(s["max_chained"], b * 2 + 1)
                wait_count(dve, s["shift_moved"], b)
                nc.vector.tensor_scalar(rounded[:, :, 0], m.negmax[:, :], -1.0, None,
                                        ALU.mult).then_inc(s["max_chained"], 1)
                dve.wait_ge(s["max_chained"], b * 2 + 2)
                nc.vector.scalar_tensor_tensor(out=rounded[:, :, 1], in0=m.negmax[:, :], scalar=-1.0,
                                               in1=m.shift[:, :, 0], op0=ALU.mult,
                                               op1=ALU.subtract).then_inc(s["shift_ready"], 1)

            def add(u, j):
                dve.wait_ge(s["probs_ready"], u * NC + vec_chunks[j + 1] + 1)
                wait_count(dve, s["vec_summed"], u * n_vec + j)
                if j == 0:
                    wait_count(dve, s["den_ready"], u)
                before = m.probs[:, vec_chunks[0] % RING, :] if j == 0 else m.sums[:, 1, :]
                nc.vector.tensor_tensor(m.sums[:, 1, :], before, m.probs[:, vec_chunks[j + 1] % RING, :],
                                        ALU.add).then_inc(s["vec_summed"], 1)

            def normalise(u):
                dve.wait_ge(s["den_ready"], u + 1)
                wait_count(dve, s["z_ready"], u)
                nc.vector.reciprocal(m.recip[0:width, :], fin[0:width, :]).then_inc(s["recip_ready"], 1)
                dve.wait_ge(s["recip_ready"], u + 1)
                dve.wait_ge(s["values_folded" if col_tiles > 1 else "values_copied"], u + 1)
                for a in range(accs):
                    values = fin[width:2 * width, :] if col_tiles > 1 else m.z[:, a, :]
                    op = nc.vector.tensor_tensor(m.z[0:width, a, :], values, m.recip[0:width, :], ALU.mult)
                op.then_inc(s["z_ready"], 1)

            def unit(u, first, last):
                for c in range(NC):
                    if not last:
                        for k in tiles_at[c]:
                            take_max(u + 1, k)
                            if k == NT - 1:
                                make_shift(u + 1)
                    for j in vec_at[c]:
                        add(u, j)
                    if c == 12 and not first:
                        normalise(u - 1)

            for k in range(NT):
                take_max(0, k)
            make_shift(0)
            units(dve, unit)
            normalise(U - 1)

        @block.gpsimd
        def _(pool):
            if cfg["shift_product"] is None:
                nc.gpsimd.memset(m.ones2[:, :].bitcast(F32), 1.0).then_inc(s["ones_ready"], 1)
            else:
                nc.gpsimd.memset(k_still[shift_row:shift_row + 2, shift_slot, :].bitcast(F32), 1.0).then_inc(s["ones_ready"], 1)

            def add(u, j):
                c = pool_chunks[j + 1]
                pool.wait_ge(s["probs_ready"], u * NC + c + 1)
                wait_count(pool, s["pool_summed"], u * n_pool + j)
                if j == 0:
                    wait_count(pool, s["den_ready"], u)
                before = m.probs[:, pool_chunks[0] % RING, :] if j == 0 else m.sums[:, 0, :]
                nc.gpsimd.tensor_tensor(m.sums[:, 0, :], before, m.probs[:, c % RING, :],
                                        ALU.add).then_inc(s["pool_summed"], 1)

            def unit(u, first, last):
                for j in range(n_pool):
                    add(u, j)

            units(pool, unit)

        @block.sync
        def _(sp):
            def load_q(dst, part, b, first_token, n, done):
                sp.dma_start(dst.bitcast(F32), m.q_dram[part, bass.ds(b // NB * dq, dq),
                                           bass.ds(b % NB * LB + first_token, n)]).then_inc(done, 16)

            def load_q_still(b, t):
                wait_count(sp, s["max_ready"], (b - 1) * NT + (t + 1) * per_row)
                for slot, r, part in cfg["q_parts"]:
                    load_q(q_still[r:r + dq, slot, t * P:(t + 1) * P], part, b, t * P, P, q_still_in[t])

            def load_q_moving(b):
                wait_count(sp, s["scores_ready"], (b - 1) * NC + 1)
                for slot, r, part in cfg["q_parts"]:
                    load_q(moving_q(b, slot, r, r + dq), part, b, 0, LB, s["q_moving_in"])

            def load_k_moving(h):
                wait_count(sp, s["max_ready"], (h - 1) * (NB * NT) + 1)
                for slot, r, part in cfg["k_parts"]:
                    sp.dma_start(k_move[r:r + dq, bass.ds(h % 2 * (ks * T) + slot * T, T)].bitcast(F32),
                                 m.k_dram[part, bass.ds(h * dq, dq), :]).then_inc(s["k_moving_in"], 16)

            def load_piece(h, t):
                wait_count(sp, s["values_done"], h * (NB * NC // 4) + (2 * (t + 1) - NC // 4))
                for slot, r, part in cfg["k_parts"]:
                    sp.dma_start(k_still[r:r + dq, slot, t * 8 * P:(t + 1) * 8 * P].bitcast(F32),
                                 m.k_dram[part, bass.ds(h * dq, dq), t * 8 * P:(t + 1) * 8 * P]).then_inc(k_still_in[t], 16)
                src = m.v_dram.rearrange("(c p) d -> p c d", p=P)[:, t * 8:(t + 1) * 8, bass.ds(h * dv, dv)]
                sp.dma_start(v_head[:, t * 8:(t + 1) * 8, :], src).then_inc(v_in[t], 16)

            def unit(u, moving, still, next_head):
                if moving:
                    load_q_moving(u + 1)
                for t in range(4):
                    if still:
                        load_q_still(u + 2, t)
                    if next_head is not None:
                        load_piece(next_head, t)

            for t in range(4):
                load_q_still(0, t)
            if H > 1:
                load_k_moving(0)
            for t in range(4):
                load_piece(0, t)
            load_q_moving(0)
            for t in range(4):
                load_q_still(1, t)
            if H > 1:
                with sp.Fori(0, H - 1) as h:
                    load_k_moving(h + 1)
                    with sp.Fori(0, NB - 1) as n:
                        unit(h * NB + n, True, True, None)
                    unit(h * NB + NB - 1, True, True, h + 1)
            with sp.Fori((H - 1) * NB, U - 2) as u:
                unit(u, True, True, None)
            unit(U - 2, True, False, None)


def finish_phase(nc, sem, m, layer, w, out):
    wt = None
    if w is not None:
        kh = w.shape[0] // P
        wt = m.probs[:, :, :].rearrange("p a b -> p (a b)")[:, 0:kh * w.shape[1]].rearrange("p (k n) -> p k n", k=kh)
    zh = 1 if layer == 3 else CH
    z_in = [m.v[:, i * 2 * LB:(i + 1) * 2 * LB].rearrange("p (k n) -> p k n", k=2) for i in range(2)]
    y = [m.v[:, (i + 2) * 2 * LB:(i + 3) * 2 * LB].rearrange("p (k n) -> p k n", k=2) for i in range(2)]
    w_in, z_loaded = sem(f"fw_in{layer}"), [sem(f"z_loaded{layer}_{i}") for i in range(2)]
    mixed, y_ready = sem(f"mixed{layer}"), sem(f"y_ready{layer}")
    z_used = mixed if layer == 0 else y_ready
    conv_done, x_done, stored = sem(f"conv_done{layer}"), sem(f"x_done{layer}"), sem(f"stored{layer}")
    mix_w, conv_w = (0, C) if layer == 0 else (None, 0)

    def block_of(pair, i):
        return pair * 2 + i

    def x_of(n):
        if layer == 0:
            return [m.x[:, k, :].rearrange("p (c j) -> p j c", j=GRID)[:, bass.ds(n * 2, 2), :] for k in range(CH)]
        return [m.x[:, k, bass.ds(n * LB, LB)] for k in range(CH)]

    with nc.Block() as block:
        @block.sync
        def _(sp):
            if w is not None:
                for k in range(kh):
                    sp.dma_start(wt[:, k, :], w[k * P:(k + 1) * P, :]).then_inc(w_in, 16)

            def pair(p):
                for i in range(2):
                    n = block_of(p, i)
                    wait_count(sp, z_used, n - 1)
                    for k in range(zh):
                        sp.dma_start(z_in[i][:, k, :], m.z_dram[k * P:(k + 1) * P, bass.ds(n * LB, LB)]).then_inc(z_loaded[i], 16)

            passes(sp, NB // 2, pair)
            if layer == 3:
                for n in range(NB):
                    sp.wait_ge(x_done, n + 1)
                    sp.dma_start(out.rearrange("(k p) n -> p k n", p=P)[:, :, n * LB:(n + 1) * LB],
                                 m.x[:, :, n * LB:(n + 1) * LB]).then_inc(stored, 16)
                sp.wait_ge(stored, 16 * NB)

        if layer != 1:
            @block.tensor
            def _(pe):
                pe.wait_ge(w_in, 16 * kh)

                def pair(p):
                    for i in range(2):
                        n = block_of(p, i)
                        if layer == 0:
                            pe.wait_ge(z_loaded[i], (p + 1) * (16 * zh))
                            wait_count(pe, y_ready, n - 1)
                            for o in range(CH):
                                for k in range(CH):
                                    mm = nc.tensor.matmul(m.psum[2 * i][:, o, :], wt[:, k, mix_w + o * P:mix_w + (o + 1) * P],
                                                          z_in[i][:, k, :], start=k == 0, stop=k == CH - 1)
                            mm.then_inc(mixed, 1)
                        pe.wait_ge(y_ready, n + 1)
                        wait_count(pe, x_done, n - 1)
                        for o in range(CH):
                            for k in range(zh):
                                mm = nc.tensor.matmul(m.psum[2 * i + 1][:, o, :], wt[:, k, conv_w + o * P:conv_w + (o + 1) * P],
                                                      y[i][:, k, :], start=k == 0, stop=k == zh - 1)
                        mm.then_inc(conv_done, 1)

                passes(pe, NB // 2, pair)

            @block.scalar
            def _(act):
                def pair(p):
                    for i in range(2):
                        n = block_of(p, i)
                        wait_count(act, conv_done, n - 1)
                        if layer == 0:
                            act.wait_ge(mixed, n + 1)
                            op = nc.scalar.activation(y[i], m.psum[2 * i][:, :, :], ACT.Copy)
                            op.then_inc(y_ready, 1)
                        else:
                            act.wait_ge(z_loaded[i], (p + 1) * (16 * zh))
                            col = {2: B_L2_V, 3: B_L3_V}[layer]
                            for k in range(zh):
                                op = nc.scalar.activation(y[i][:, k, :], z_in[i][:, k, :], ACT.Identity,
                                                          bias=m.bias[:, col + k:col + k + 1])
                            op.then_inc(y_ready, 1)

                passes(act, NB // 2, pair)

        @block.vector
        def _(dve):
            def pair(p):
                for i in range(2):
                    n = block_of(p, i)
                    if layer == 1:
                        dve.wait_ge(z_loaded[i], (p + 1) * (16 * zh))
                        wait_count(dve, x_done, n - 1)
                        for k in range(CH):
                            op = nc.vector.tensor_scalar(y[i][:, k, :], z_in[i][:, k, :], m.bias[:, B_L1_V + k:B_L1_V + k + 1],
                                                         m.bias[:, B_GAMMA:B_GAMMA + 1], ALU.add, ALU.mult)
                        op.then_inc(y_ready, 1)
                        dve.wait_ge(y_ready, n + 1)
                    else:
                        dve.wait_ge(conv_done, n + 1)
                    for k, xk in enumerate(x_of(n)):
                        if layer == 0:
                            op = nc.vector.tensor_tensor(xk, m.psum[2 * i + 1][:, k, :].rearrange("p (j c) -> p j c", j=2),
                                                         xk, ALU.add)
                        elif layer == 1:
                            op = nc.vector.tensor_tensor(xk, y[i][:, k, :], xk, ALU.add)
                        else:
                            col = {2: B_L2_O, 3: B_L3_O}[layer] + k
                            op = nc.vector.scalar_tensor_tensor(out=xk, in0=m.psum[2 * i + 1][:, k, :],
                                                                scalar=m.bias[:, col:col + 1], in1=xk,
                                                                op0=ALU.add, op1=ALU.add)
                    op.then_inc(x_done, 1)

            passes(dve, NB // 2, pair)


def build(nc, x, bias, const, proj0, proj1, proj2, proj3, fin0, fin2, fin3, out):
    with ExitStack() as ctx:
        m = Memory(nc, ctx)
        held = []

        def sem(name):
            held.append(nc.alloc_semaphore(name=name))
            return held[-1]

        load_phase(nc, sem, m, x, bias, const)
        for layer, (proj, fin) in enumerate(((proj0, fin0), (proj1, None), (proj2, fin2), (proj3, fin3))):
            project_phase(nc, sem, m, layer, proj)
            attention_phase(nc, sem, m, layer)
            finish_phase(nc, sem, m, layer, fin, out)
            nc.clear_and_free_semaphores(held)
            nc.all_engine_barrier()
            held.clear()


def _bias_table(np, i):
    table = np.zeros((P, B_COLS), np.float32)
    table[0:32, B_L1_QK] = i["L1_conv_bk"]
    table[32:64, B_L1_QK] = i["L1_conv_bq"]
    table[:, B_GAMMA] = i["L1_conv_gamma"][0]
    for col, name in ((B_L1_V, "L1_conv_bv"), (B_L2_Q, "L2_conv_bq"), (B_L2_K, "L2_conv_bk"), (B_L2_V, "L2_conv_bv"),
                      (B_L2_O, "L2_conv_bo"), (B_L3_O, "L3_conv_W_b")):
        table[:, col:col + 2] = i[name].reshape(2, P).T
    for col, name in ((B_L3_Q, "L3_conv_theta_b"), (B_L3_K, "L3_conv_phi_b"), (B_L3_V, "L3_conv_g_b")):
        table[:, col] = i[name]
    return table


def _const_table(np):
    eye = np.eye(P, dtype=np.float32)
    sum32 = np.tile(np.eye(32, dtype=np.float32), (4, 1))
    sum64 = np.tile(np.eye(64, dtype=np.float32), (2, 1))
    return np.concatenate([eye, np.ones((P, P), np.float32), sum32, sum64], axis=1)


def kernel(**inputs):
    import numpy as np
    import concourse.bacc as bacc
    from concourse.bass_utils import run_bass_kernel_spmd

    i = {k: np.asarray(v) for k, v in inputs.items()}

    def side_by_side(*names):
        return np.ascontiguousarray(np.concatenate([i[n].T for n in names], axis=1))

    arrays = {
        "x": np.ascontiguousarray(i["x"].reshape(C, T)),
        "bias": _bias_table(np, i),
        "const": _const_table(np),
        "proj0": side_by_side("L0_conv_Wf", "L0_conv_Wg", "L0_conv_Wh"),
        "proj1": side_by_side("L1_conv_wk", "L1_conv_wq", "L1_conv_wv"),
        "proj2": side_by_side("L2_conv_Wq", "L2_conv_Wk", "L2_conv_Wv"),
        "proj3": side_by_side("L3_conv_theta_w", "L3_conv_phi_w", "L3_conv_g_w"),
        "fin0": side_by_side("L0_conv_Wm", "L0_conv_Wv"),
        "fin2": side_by_side("L2_conv_Wo"),
        "fin3": side_by_side("L3_conv_W_w"),
    }
    nc = bacc.Bacc("TRN2", target_bir_lowering=False, num_devices=1)
    args = {n: nc.dram_tensor(f"in_{n}", a.shape, F32, kind="ExternalInput").ap() for n, a in arrays.items()}
    out = nc.dram_tensor("out_x", (C, T), F32, kind="ExternalOutput").ap()
    build(nc, out=out, **args)
    r = run_bass_kernel_spmd(nc, [{f"in_{n}": a for n, a in arrays.items()}], core_ids=[0])
    return r.results[0]["out_x"].reshape(1, C, 64, 64)
```

```python
import concourse.bass as bass
from concourse import mybir
from contextlib import ExitStack

F32 = mybir.dt.float32
F32R = mybir.dt.float32r
ALU = mybir.AluOpType
ACT = mybir.ActivationFunctionType
AX = mybir.AxisListType

C, T, P = 256, 4096, 128
CH = C // P
LB = 512
NB = T // LB
NC = T // P
GRID = 16
RING = 8

STACK32 = dict(q_parts=((0, 0, 0), (0, 32, 1), (0, 64, 0)), k_parts=((0, 0, 0), (0, 32, 0), (0, 64, 1)),
               products=((0, 0, 96),), shift=(0, 96), shift_product=0, k_slots=1, q_slots=1)
STACK64 = dict(q_parts=((0, 0, 0), (0, 64, 1), (1, 0, 0)), k_parts=((0, 0, 0), (0, 64, 0), (1, 0, 1)),
               products=((0, 0, 128), (1, 1, 64)), shift=(1, 64), shift_product=1, k_slots=2, q_slots=2)
STACK128 = dict(q_parts=((0, 0, 0), (1, 0, 1)), k_parts=((0, 0, 0), (1, 0, 1)),
                products=((0, 0, 128), (0, 1, 128), (1, 0, 128)), shift=(2, 0), shift_product=None,
                k_slots=2, q_slots=2)
PE_GROUPS = (1, 3, 5, 7)
NOT_PE = tuple(c for c in range(NC) if c // 4 not in PE_GROUPS)
EVEN = tuple(range(0, NC, 2))
LAYERS = (
    dict(heads=8, dq=32, dv=32, scale=32 ** -0.5, pe_groups=PE_GROUPS, pool_chunks=NOT_PE, **STACK32),
    dict(heads=1, dq=32, dv=256, scale=1.0, pe_groups=(), pool_chunks=EVEN, **STACK32),
    dict(heads=4, dq=64, dv=64, scale=64 ** -0.5, pe_groups=(), pool_chunks=EVEN, **STACK64),
    dict(heads=1, dq=128, dv=128, scale=1.0, pe_groups=(), pool_chunks=EVEN, **STACK128),
)

B_L1_QK, B_L1_V, B_GAMMA, B_L2_Q, B_L2_K, B_L2_V, B_L2_O = 0, 1, 3, 4, 6, 8, 10
B_L3_Q, B_L3_K, B_L3_V, B_L3_O, B_ZERO, B_COLS = 12, 13, 14, 15, 17, 18
K_IDENT, K_ONES, K_SUM32, K_SUM64, K_COLS = 0, P, 2 * P, 2 * P + 32, 2 * P + 96


def wait_count(eng, sem, value):
    if isinstance(value, int) and value <= 0:
        return
    eng.wait_ge(sem, value)


class Memory:

    def __init__(self, nc, ctx):
        def sb(name, shape, dt=F32):
            return ctx.enter_context(nc.sbuf_tensor(name, shape, dt))

        self.x = sb("x", [P, CH, T])
        self.qk = sb("qk", [P, 27 * 1024], F32R)
        self.v = sb("v", [P, 8192])
        self.probs = sb("probs", [P, RING, LB])
        self.sums = sb("sums", [P, 2, 2, LB])
        self.total = sb("total", [P, LB])
        self.z = sb("z", [P, 2, LB])
        self.recip = sb("recip", [P, LB])
        self.bias = sb("bias", [P, B_COLS])
        self.const = sb("const", [P, K_COLS])
        self.rowmax = sb("rowmax", [P, 4, NB])
        self.negmax = sb("negmax", [P, 4])
        self.shift = sb("shift", [P, 4, 2])
        self.ones2 = sb("ones2", [2, P], F32R)
        self.psum = [ctx.enter_context(nc.psum_tensor(f"bank{i}", [P, 2, LB], F32)) for i in range(4)]

        def dram(name, shape, dt):
            return nc.dram_tensor(name, shape, dt, kind="Internal").ap()

        self.q_dram = dram("q_dram", (2, C, T), F32)
        self.k_dram = dram("k_dram", (2, C, T), F32)
        self.v_dram = dram("v_dram", (T, C), F32)
        self.z_dram = dram("z_dram", (C, T), F32)

    def bank(self, i):
        return self.psum[i // 2][:, i % 2, :]


def load_phase(nc, sem, m, x, bias, const):
    loaded = sem("inputs_loaded")
    with nc.Block() as block:
        @block.sync
        def _(sp):
            for half in range(CH):
                sp.dma_start(m.x[:, half, :], x[half * P:(half + 1) * P, :]).then_inc(loaded, 16)
            sp.dma_start(m.bias[:, :], bias).then_inc(loaded, 16)
            sp.dma_start(m.const[:, :], const).then_inc(loaded, 16)
            sp.wait_ge(loaded, 64)


def weights_view(m, cols):
    return m.probs[:, :, :].rearrange("p a b -> p (a b)")[:, 0:CH * cols].rearrange("p (k n) -> p k n", k=CH)


def passes(eng, trips, body):
    body(0)
    if trips > 1:
        with eng.Fori(1, trips) as trip:
            body(trip)


def project_phase(nc, sem, m, layer, w):
    cfg = LAYERS[layer]
    cols = w.shape[1]
    wt = weights_view(m, cols)
    hi = [m.qk[:, s * LB:(s + 1) * LB] for s in range(4)]
    lo = [m.qk[:, (4 + s) * LB:(5 + s) * LB] for s in range(4)]
    vs = [m.v[:, s * LB:(s + 1) * LB] for s in range(4)]
    w_loaded = sem(f"w_loaded{layer}")
    qk_done, hi_done, lo_done = sem(f"qk_done{layer}"), sem(f"hi_done{layer}"), sem(f"lo_done{layer}")
    v_done, v_copied = sem(f"v_done{layer}"), sem(f"v_copied{layer}")
    qk_stored = [sem(f"qk_stored{layer}_{s}") for s in range(4)]
    v_stored = [sem(f"v_stored{layer}_{s}") for s in range(4)]

    groups, rows = ((2, P), (1, 64), (4, P), (2, P))[layer]
    trips, body = ((1, 32), (2, 4), (4, 8), (4, 4))[layer]
    trip_px = body // groups * LB
    stores = (4, 4, 2, 2)[layer]
    v_trips, v_body = (4, 4) if layer == 0 else (1, NC)
    v_col = (2 * C, 64, 2 * C, C)[layer]
    v_n = LB if layer == 0 else cfg["heads"] * cfg["dv"]

    def bias_of(i):
        col = (B_ZERO, B_L1_QK, B_L2_Q + i % groups, B_L3_Q + i % groups)[layer]
        return m.bias[0:rows, col:col + 1]

    with nc.Block() as block:
        @block.tensor
        def _(pe):
            pe.wait_ge(w_loaded, 16 * CH)

            def qk_tiles(trip):
                for i in range(body):
                    wait_count(pe, lo_done, trip * body + i - 3)
                    for k in range(CH):
                        if layer == 0:
                            lhs, rhs = m.x[:, k, i * P:(i + 1) * P], wt[:, k, 0:LB]
                        else:
                            lhs = wt[:, k, i % groups * rows:(i % groups + 1) * rows]
                            rhs = m.x[:, k, bass.ds(trip * trip_px + i // groups * LB, LB)]
                        mm = nc.tensor.matmul(m.bank(i % 4)[0:rows, :], lhs, rhs, start=k == 0, stop=k == CH - 1)
                    mm.then_inc(qk_done, 1)

            def v_tiles(trip):
                for i in range(v_body):
                    wait_count(pe, v_copied, trip * v_body + i - 3)
                    for k in range(CH):
                        if layer == 0:
                            lhs = wt[:, k, v_col + i % CH * P:v_col + (i % CH + 1) * P]
                            rhs = m.x[:, k, bass.ds(trip * (2 * LB) + i // CH * LB, LB)]
                        else:
                            lhs, rhs = m.x[:, k, i * P:(i + 1) * P], wt[:, k, v_col:v_col + v_n]
                        mm = nc.tensor.matmul(m.bank(4 + i % 4)[:, 0:v_n], lhs, rhs, start=k == 0, stop=k == CH - 1)
                    mm.then_inc(v_done, 1)

            passes(pe, trips, qk_tiles)
            passes(pe, v_trips, v_tiles)

        @block.scalar
        def _(act):
            def round_hi(trip):
                for i in range(body):
                    act.wait_ge(qk_done, trip * body + i + 1)
                    wait_count(act, qk_stored[i % 4], (trip * (body // 4) + i // 4) * (16 * stores))
                    nc.scalar.activation(hi[i % 4][0:rows, :], m.bank(i % 4)[0:rows, :], ACT.Identity,
                                         bias=bias_of(i)).then_inc(hi_done, 1)

            passes(act, trips, round_hi)

        @block.vector
        def _(dve):
            def round_lo(trip):
                for i in range(body):
                    dve.wait_ge(hi_done, trip * body + i + 1)
                    nc.vector.scalar_tensor_tensor(out=lo[i % 4][0:rows, :], in0=m.bank(i % 4)[0:rows, :],
                                                   scalar=bias_of(i), in1=hi[i % 4][0:rows, :],
                                                   op0=ALU.add, op1=ALU.subtract).then_inc(lo_done, 1)

            def copy_v(trip):
                for i in range(v_body):
                    dve.wait_ge(v_done, trip * v_body + i + 1)
                    wait_count(dve, v_stored[i % 4], (trip * (v_body // 4) + i // 4) * 16)
                    nc.vector.tensor_copy(vs[i % 4][:, 0:v_n], m.bank(4 + i % 4)[:, 0:v_n]).then_inc(v_copied, 1)

            passes(dve, trips, round_lo)
            passes(dve, v_trips, copy_v)

        @block.sync
        def _(sp):
            for k in range(CH):
                sp.dma_start(wt[:, k, :], w[k * P:(k + 1) * P, :]).then_inc(w_loaded, 16)

            def store_qk(trip):
                for i in range(body):
                    sp.wait_ge(lo_done, trip * body + i + 1)
                    for part, tile in enumerate((hi[i % 4], lo[i % 4])):
                        if layer == 0:
                            at = (slice(i % 2 * P, (i % 2 + 1) * P), slice(i // 2 * C, (i // 2 + 1) * C))
                            moves = ((m.q_dram[part][at], tile[:, 0:C]), (m.k_dram[part][at], tile[:, C:2 * C]))
                        else:
                            px = bass.ds(trip * trip_px + i // groups * LB, LB)
                            if layer == 1:
                                moves = ((m.q_dram[part, 0:32, px], tile[0:32, :]), (m.k_dram[part, 0:32, px], tile[32:64, :]))
                            else:
                                g = i % groups
                                half = g % (groups // 2) * P
                                to = m.q_dram if g < groups // 2 else m.k_dram
                                moves = ((to[part, half:half + P, px], tile[:, :]),)
                        for dst, src in moves:
                            sp.dma_start(dst, src.bitcast(F32)).then_inc(qk_stored[i % 4], 16)

            v_tokens = m.v_dram.rearrange("(j h p) n -> h p j n", h=CH, p=P)

            def store_v(trip):
                for i in range(v_body):
                    sp.wait_ge(v_copied, trip * v_body + i + 1)
                    if layer == 0:
                        dst = v_tokens[i % CH][:, bass.ds(trip * 4 + i // CH * 2, 2), :]
                        src = vs[i % 4].rearrange("p (j n) -> p j n", j=2)
                    else:
                        dst, src = m.v_dram[i * P:(i + 1) * P, 0:v_n], vs[i % 4][:, 0:v_n]
                    sp.dma_start(dst, src).then_inc(v_stored[i % 4], 16)

            passes(sp, trips, store_qk)
            passes(sp, v_trips, store_v)
            for s in range(4):
                sp.wait_ge(qk_stored[s], trips * (body // 4) * 16 * stores)
                sp.wait_ge(v_stored[s], v_trips * (v_body // 4) * 16)


def attention_phase(nc, sem, m, layer):
    cfg = LAYERS[layer]
    H, dq, dv, products = cfg["heads"], cfg["dq"], cfg["dv"], cfg["products"]
    ks, qs = cfg["k_slots"], cfg["q_slots"]
    U = H * NB
    NT, per_row = 4 * T // LB, T // LB
    accs = -(-dv // P)
    width = min(dv, P)
    col_tiles = P // width
    shift_slot, shift_row = cfg["shift"]
    b_slots = max(qs, shift_slot + 1)
    n_q, n_k = len(cfg["q_parts"]), len(cfg["k_parts"])
    pool_chunks = cfg["pool_chunks"]
    pe_groups = cfg["pe_groups"]
    vec_chunks = tuple(c for c in range(NC) if c not in pool_chunks and c // 4 not in pe_groups)
    n_pool, n_vec = len(pool_chunks) - 1, max(len(vec_chunks) - 1, 0)
    group = col_tiles
    groups = NC // group
    FOLD_TILE, FOLD_AT, INVERT_AT = 13, 11, (14, 17, 20, 23)
    ADD_AT = 7
    copy_at = {1: 0, 2: 2, 4: 4}[group]
    fold_bank, shift_bank = m.bank(FOLD_TILE % 3), m.bank(3 + NC % 3)
    tiles_at = [[k for k in range(NT) if k * 29 // NT == c] for c in range(NC)]
    vec_at = [[j for j in range(n_vec) if min(vec_chunks[j + 1] + 2, NC - 1) == c] for c in range(NC)]

    at = 0

    def take(n):
        nonlocal at
        at += n
        return m.qk[:, at - n:at]

    k_still = take(ks * T).rearrange("p (s n) -> p s n", s=ks)
    k_move = take(2 * ks * T) if H > 1 else None
    q_still = take(qs * LB).rearrange("p (s n) -> p s n", s=qs)
    q_move = take(2 * b_slots * LB)
    v_head = m.v[:, 0:NC * dv].rearrange("p (c d) -> p c d", c=NC)
    rounded = m.shift[:, :, :].bitcast(F32R)

    def score_bank(c):
        return m.bank(3 + c % 3)

    def sum_step(chunks, engine, j):
        early, whole = m.sums[:, engine, 0, :], m.sums[:, engine, 1, :]
        n_early = len([c for c in chunks[1:] if c < FOLD_AT])
        before = m.probs[:, chunks[0] % RING, :] if j == 0 else early if j <= n_early else whole
        return early if j < n_early else whole, before, m.probs[:, chunks[j + 1] % RING, :]

    def moving_q(u, slot, r0, r1):
        return q_move[r0:r1, bass.ds(u % 2 * (b_slots * LB) + slot * LB, LB)]

    def moving_k(b, slot, rows, col):
        if H == 1:
            return k_still[0:rows, slot, col:col + LB]
        return k_move[0:rows, bass.ds(b // NB % 2 * (ks * T) + slot * T + col, LB)]

    def max_bank(k):
        return m.bank((k if k < FOLD_TILE else k + 1) % 3)

    pe_sum = m.bank(7)
    acc = [m.bank(6), m.bank(7)][0:accs]

    s = {n: sem(f"{n}{layer}") for n in (
        "ones_ready", "max_ready", "max_taken", "max_chained", "shift_ready", "shift_moved", "shift_copied",
        "scores_ready", "probs_ready", "values_done", "values_copied", "pe_summed", "sum_copied", "pool_summed", "vec_summed",
        "totals", "den_ready", "den_copied", "inverted", "z_ready", "z_stored", "k_moving_in", "q_moving_in")}
    q_still_in = [sem(f"q_still_in{layer}_{t}") for t in range(4)]
    k_still_in = [sem(f"k_still_in{layer}_{t}") for t in range(4)]
    v_in = [sem(f"v_in{layer}_{t}") for t in range(4)]

    def units(eng, unit):
        unit(0, True, False)
        with eng.Fori(1, U - 1) as u:
            unit(u, False, False)
        unit(U - 1, False, True)

    with nc.Block() as block:
        @block.tensor
        def _(pe):
            def max_tile(b, k):
                t, part = k // per_row, k % per_row
                if k == 0:
                    if H > 1:
                        pe.wait_ge(s["k_moving_in"], (b // NB + 1) * (16 * n_k))
                    elif isinstance(b, int) and b == 0:
                        for piece in range(4):
                            pe.wait_ge(k_still_in[piece], 16 * n_k)
                if part == 0:
                    pe.wait_ge(q_still_in[t], (b + 1) * (16 * n_q))
                if k == FOLD_TILE + 2:
                    wait_count(pe, s["den_copied"], b - 1)
                else:
                    wait_count(pe, s["max_taken"], b * NT + k - (1 if k in (FOLD_TILE, FOLD_TILE + 1) else 2))
                for i, (sk, sq, rows) in enumerate(products):
                    mm = nc.tensor.matmul(max_bank(k), q_still[0:rows, sq, t * P:(t + 1) * P],
                                          moving_k(b, sk, rows, part * LB), start=i == 0, stop=i == len(products) - 1)
                mm.then_inc(s["max_ready"], 1)

            def shift_rows(b):
                pe.wait_ge(s["shift_ready"], b + 1)
                wait_count(pe, s["probs_ready"], b * NC - 2)
                for t in range(4):
                    mm = nc.tensor.matmul(shift_bank[0:2, t * P:(t + 1) * P], m.shift[:, t, :],
                                          m.const[:, K_IDENT:K_IDENT + P], start=True, stop=True)
                mm.then_inc(s["shift_moved"], 1)

            def scores(u, c):
                if c == 0:
                    pe.wait_ge(s["shift_copied"], u + 1)
                    pe.wait_ge(s["q_moving_in"], (u + 1) * (16 * n_q))
                if c % 8 == 0:
                    pe.wait_ge(k_still_in[c // 8], (u // NB + 1) * (16 * n_k))
                if c != 2:
                    wait_count(pe, s["probs_ready"], u * NC + (c - 1 if c < 2 else c - 2))
                out = score_bank(c)
                for i, (sk, sq, rows) in enumerate(products):
                    rows += 2 * (i == cfg["shift_product"])
                    last = i == len(products) - 1 and cfg["shift_product"] is not None
                    mm = nc.tensor.matmul(out, k_still[0:rows, sk, c * P:(c + 1) * P], moving_q(u, sq, 0, rows),
                                          start=i == 0, stop=last)
                if cfg["shift_product"] is None:
                    mm = nc.tensor.matmul(out, m.ones2[:, :], moving_q(u, shift_slot, 0, 2), start=False, stop=True)
                mm.then_inc(s["scores_ready"], 1)

            def values(u, g):
                pe.wait_ge(s["probs_ready"], u * NC + group * (g + 1))
                if g == 0:
                    wait_count(pe, s["values_copied"], u)
                if g * group % 8 == 0:
                    pe.wait_ge(v_in[g * group // 8], (u // NB + 1) * 16)
                for c in range(group * g, group * (g + 1)):
                    r = c % group * width
                    for a in range(accs):
                        mm = nc.tensor.matmul(acc[a][r:r + width, :], v_head[:, c, a * P:a * P + width],
                                              m.probs[:, c % RING, :], start=c < group, stop=c >= NC - group)
                mm.then_inc(s["values_done"], 1)

            def sum_probs(u, g):
                if g == pe_groups[0]:
                    wait_count(pe, s["sum_copied"], u)
                for c in range(group * g, group * (g + 1)):
                    r = c % group * width
                    mm = nc.tensor.matmul(pe_sum[r:r + width, :], m.const[:, K_SUM32:K_SUM32 + width],
                                          m.probs[:, c % RING, :], start=g == pe_groups[0], stop=g == pe_groups[-1])
                mm.then_inc(s["pe_summed"], 1)

            def denominators(u):
                pe.wait_ge(s["totals"], u + 1)
                pe.wait_ge(s["values_copied"], u + 1)
                if not (isinstance(u, int) and u >= U - 2):
                    pe.wait_ge(s["max_taken"], (u + 2) * NT + FOLD_TILE - 2)
                mm = nc.tensor.matmul(fold_bank[0:width, :], m.const[:, K_ONES:K_ONES + width], m.total[:, :],
                                      start=True, stop=True)
                if col_tiles > 1:
                    k = K_SUM32 if width == 32 else K_SUM64
                    mm = nc.tensor.matmul(fold_bank[width:2 * width, :], m.const[:, k:k + width], m.z[:, 0, :],
                                          start=True, stop=True)
                mm.then_inc(s["den_ready"], 1)

            def unit(u, first, last):
                for c in range(NC):
                    if c > 0:
                        scores(u, c)
                    if not last:
                        for k in tiles_at[c]:
                            if k == FOLD_TILE and not first:
                                denominators(u - 1)
                            max_tile(u + 1, k)
                    elif c == FOLD_AT:
                        denominators(u - 1)
                    if c == 0:
                        scores(u, c)
                    if c == NC - 1 and not last:
                        shift_rows(u + 1)
                    if (c + 1) % group == 0:
                        g = c // group
                        if g > 0:
                            values(u, g - 1)
                        elif not first:
                            values(u - 1, groups - 1)
                    if c % 4 == 0 and c > 4 and c // 4 - 2 in pe_groups:
                        sum_probs(u, c // 4 - 2)
                    if c in (0, 4) and c // 4 + 6 in pe_groups and not first:
                        sum_probs(u - 1, c // 4 + 6)

            pe.wait_ge(s["ones_ready"], 1)
            for k in range(NT):
                max_tile(0, k)
            shift_rows(0)
            units(pe, unit)
            if pe_groups and pe_groups[-2] == 6:
                sum_probs(U - 1, 6)
            values(U - 1, groups - 1)
            if pe_groups and pe_groups[-1] == 7:
                sum_probs(U - 1, 7)
            denominators(U - 1)

        @block.scalar
        def _(act):
            def copy_shift(u):
                act.wait_ge(s["shift_moved"], u + 1)
                nc.scalar.activation(moving_q(u, shift_slot, shift_row, shift_row + 2), shift_bank[0:2, :],
                                     ACT.Copy).then_inc(s["shift_copied"], 1)

            def free_probs(u, c):
                if c % group == 0:
                    wait_count(act, s["values_done"], u * groups + (c - RING) // group + 1)
                before = c - RING
                uu = u if before >= 0 else u - 1
                before %= NC
                if before in pool_chunks:
                    wait_count(act, s["pool_summed"], uu * n_pool + max(pool_chunks.index(before), 1))
                elif before // 4 in pe_groups:
                    wait_count(act, s["pe_summed"], uu * len(pe_groups) + pe_groups.index(before // 4) + 1)
                else:
                    wait_count(act, s["vec_summed"], uu * n_vec + max(vec_chunks.index(before), 1))

            def copy_values(u):
                act.wait_ge(s["values_done"], (u + 1) * groups)
                wait_count(act, s["z_stored"], u * (16 * accs))
                for a in range(accs):
                    op = nc.scalar.activation(m.z[:, a, :], acc[a], ACT.Copy)
                op.then_inc(s["values_copied"], 1)

            def copy_sum(u):
                act.wait_ge(s["pe_summed"], (u + 1) * len(pe_groups))
                wait_count(act, s["totals"], u)
                nc.scalar.activation(m.sums[:, 1, 1, :], pe_sum, ACT.Copy).then_inc(s["sum_copied"], 1)

            def copy_denominators(u):
                act.wait_ge(s["den_ready"], u + 1)
                wait_count(act, s["z_ready"], u)
                op = nc.scalar.activation(m.recip[0:width, :], fold_bank[0:width, :], ACT.Copy)
                if col_tiles > 1:
                    op = nc.scalar.activation(m.z[0:width, 0, :], fold_bank[width:2 * width, :], ACT.Copy)
                op.then_inc(s["den_copied"], 1)

            def store_z(u):
                act.wait_ge(s["z_ready"], u + 1)
                for a in range(accs):
                    act.dma_start(m.z_dram[bass.ds(u // NB * dv + a * P, width), bass.ds(u % NB * LB, LB)],
                                  m.z[0:width, a, :]).then_inc(s["z_stored"], 16)

            def unit(u, first, last):
                for c in range(NC):
                    act.wait_ge(s["scores_ready"], u * NC + c + 1)
                    free_probs(u, c)
                    nc.scalar.activation(m.probs[:, c % RING, :], score_bank(c), ACT.Exp,
                                         scale=cfg["scale"]).then_inc(s["probs_ready"], 1)
                    if c == copy_at and not first:
                        copy_values(u - 1)
                    if c == 6 and pe_groups and not first:
                        copy_sum(u - 1)
                    if c == FOLD_AT and not first:
                        copy_denominators(u - 1)
                    if c == 30 and not first:
                        store_z(u - 1)
                if not last:
                    copy_shift(u + 1)

            copy_shift(0)
            units(act, unit)
            copy_values(U - 1)
            if pe_groups:
                copy_sum(U - 1)
            copy_denominators(U - 1)
            store_z(U - 1)
            act.wait_ge(s["z_stored"], U * 16 * accs)

        @block.vector
        def _(dve):
            def take_max(b, k):
                dve.wait_ge(s["max_ready"], b * NT + k + 1)
                if k == 0:
                    wait_count(dve, s["shift_ready"], b)
                nc.vector.reduce_max(m.rowmax[:, k // per_row, k % per_row:k % per_row + 1], max_bank(k),
                                     AX.X).then_inc(s["max_taken"], 1)

            def make_shift(b):
                dve.wait_ge(s["max_taken"], (b + 1) * NT)
                nc.vector.reduce_max(m.negmax[:, :], m.rowmax[:, :, :], AX.X).then_inc(s["max_chained"], 1)
                dve.wait_ge(s["max_chained"], b * 2 + 1)
                wait_count(dve, s["shift_moved"], b)
                nc.vector.tensor_scalar(rounded[:, :, 0], m.negmax[:, :], -1.0, None,
                                        ALU.mult).then_inc(s["max_chained"], 1)
                dve.wait_ge(s["max_chained"], b * 2 + 2)
                nc.vector.scalar_tensor_tensor(out=rounded[:, :, 1], in0=m.negmax[:, :], scalar=-1.0,
                                               in1=m.shift[:, :, 0], op0=ALU.mult,
                                               op1=ALU.subtract).then_inc(s["shift_ready"], 1)

            def add(u, j):
                out, before, tile_in = sum_step(vec_chunks, 1, j)
                dve.wait_ge(s["probs_ready"], u * NC + vec_chunks[j + 1] + 1)
                wait_count(dve, s["vec_summed"], u * n_vec + j)
                wait_count(dve, s["totals"], u if vec_chunks[j + 1] >= FOLD_AT else 0)
                nc.vector.tensor_tensor(out, before, tile_in, ALU.add).then_inc(s["vec_summed"], 1)

            def invert(u, piece):
                dve.wait_ge(s["den_copied"], u + 1)
                part = m.recip[0:width, piece * P:(piece + 1) * P]
                nc.vector.reciprocal(part, part).then_inc(s["inverted"], 1)

            def unit(u, first, last):
                for c in range(NC):
                    if not last:
                        for k in tiles_at[c]:
                            take_max(u + 1, k)
                            if k == NT - 1:
                                make_shift(u + 1)
                    for j in vec_at[c]:
                        add(u, j)
                    if c in INVERT_AT and not first:
                        invert(u - 1, INVERT_AT.index(c))

            for k in range(NT):
                take_max(0, k)
            make_shift(0)
            units(dve, unit)
            for piece in range(4):
                invert(U - 1, piece)

        @block.gpsimd
        def _(pool):
            if cfg["shift_product"] is None:
                nc.gpsimd.memset(m.ones2[:, :].bitcast(F32), 1.0).then_inc(s["ones_ready"], 1)
            else:
                nc.gpsimd.memset(k_still[shift_row:shift_row + 2, shift_slot, :].bitcast(F32), 1.0).then_inc(s["ones_ready"], 1)

            def add(u, j):
                out, before, tile_in = sum_step(pool_chunks, 0, j)
                pool.wait_ge(s["probs_ready"], u * NC + pool_chunks[j + 1] + 1)
                wait_count(pool, s["pool_summed"], u * n_pool + j)
                if pool_chunks[j + 1] >= FOLD_AT:
                    wait_count(pool, s["totals"], u)
                nc.gpsimd.tensor_tensor(out, before, tile_in, ALU.add).then_inc(s["pool_summed"], 1)

            def add_engines(u):
                pool.wait_ge(s["pool_summed"], (u + 1) * n_pool)
                if pe_groups:
                    pool.wait_ge(s["sum_copied"], u + 1)
                else:
                    pool.wait_ge(s["vec_summed"], (u + 1) * n_vec)
                wait_count(pool, s["den_ready"], u)
                nc.gpsimd.tensor_tensor(m.total[:, :], m.sums[:, 0, 1, :], m.sums[:, 1, 1, :],
                                        ALU.add).then_inc(s["totals"], 1)

            def normalise(u):
                pool.wait_ge(s["inverted"], 4 * (u + 1))
                for a in range(accs):
                    op = nc.gpsimd.tensor_tensor(m.z[0:width, a, :], m.z[0:width, a, :], m.recip[0:width, :], ALU.mult)
                op.then_inc(s["z_ready"], 1)

            def unit(u, first, last):
                for j in range(n_pool):
                    if not first:
                        if pool_chunks[j] <= ADD_AT < pool_chunks[j + 1]:
                            add_engines(u - 1)
                        if pool_chunks[j] <= 24 < pool_chunks[j + 1]:
                            normalise(u - 1)
                    add(u, j)

            units(pool, unit)
            add_engines(U - 1)
            normalise(U - 1)

        @block.sync
        def _(sp):
            def load_q(dst, part, b, first_token, n, done):
                sp.dma_start(dst.bitcast(F32), m.q_dram[part, bass.ds(b // NB * dq, dq),
                                           bass.ds(b % NB * LB + first_token, n)]).then_inc(done, 16)

            def load_q_still(b, t):
                wait_count(sp, s["max_ready"], (b - 1) * NT + (t + 1) * per_row)
                for slot, r, part in cfg["q_parts"]:
                    load_q(q_still[r:r + dq, slot, t * P:(t + 1) * P], part, b, t * P, P, q_still_in[t])

            def load_q_moving(b):
                wait_count(sp, s["scores_ready"], (b - 1) * NC + 1)
                for slot, r, part in cfg["q_parts"]:
                    load_q(moving_q(b, slot, r, r + dq), part, b, 0, LB, s["q_moving_in"])

            def load_k_moving(h):
                wait_count(sp, s["max_ready"], (h - 1) * (NB * NT) + 1)
                for slot, r, part in cfg["k_parts"]:
                    sp.dma_start(k_move[r:r + dq, bass.ds(h % 2 * (ks * T) + slot * T, T)].bitcast(F32),
                                 m.k_dram[part, bass.ds(h * dq, dq), :]).then_inc(s["k_moving_in"], 16)

            def load_piece(h, t):
                wait_count(sp, s["values_done"], h * (NB * groups) + ((t + 1) * (groups // 4) - groups))
                for slot, r, part in cfg["k_parts"]:
                    sp.dma_start(k_still[r:r + dq, slot, t * 8 * P:(t + 1) * 8 * P].bitcast(F32),
                                 m.k_dram[part, bass.ds(h * dq, dq), t * 8 * P:(t + 1) * 8 * P]).then_inc(k_still_in[t], 16)
                src = m.v_dram.rearrange("(c p) d -> p c d", p=P)[:, t * 8:(t + 1) * 8, bass.ds(h * dv, dv)]
                sp.dma_start(v_head[:, t * 8:(t + 1) * 8, :], src).then_inc(v_in[t], 16)

            def unit(u, moving, still, next_head):
                if moving:
                    load_q_moving(u + 1)
                for t in range(4):
                    if still:
                        load_q_still(u + 2, t)
                    if next_head is not None:
                        load_piece(next_head, t)

            for t in range(4):
                load_q_still(0, t)
            if H > 1:
                load_k_moving(0)
            for t in range(4):
                load_piece(0, t)
            load_q_moving(0)
            for t in range(4):
                load_q_still(1, t)
            if H > 1:
                with sp.Fori(0, H - 1) as h:
                    load_k_moving(h + 1)
                    with sp.Fori(0, NB - 1) as n:
                        unit(h * NB + n, True, True, None)
                    unit(h * NB + NB - 1, True, True, h + 1)
            with sp.Fori((H - 1) * NB, U - 2) as u:
                unit(u, True, True, None)
            unit(U - 2, True, False, None)


def finish_phase(nc, sem, m, layer, w, out):
    wt = None
    if w is not None:
        kh = w.shape[0] // P
        wt = m.probs[:, :, :].rearrange("p a b -> p (a b)")[:, 0:kh * w.shape[1]].rearrange("p (k n) -> p k n", k=kh)
    zh = 1 if layer == 3 else CH
    z_in = [m.v[:, i * 2 * LB:(i + 1) * 2 * LB].rearrange("p (k n) -> p k n", k=2) for i in range(2)]
    y = [m.v[:, (i + 2) * 2 * LB:(i + 3) * 2 * LB].rearrange("p (k n) -> p k n", k=2) for i in range(2)]
    w_in, z_loaded = sem(f"fw_in{layer}"), [sem(f"z_loaded{layer}_{i}") for i in range(2)]
    mixed, y_ready = sem(f"mixed{layer}"), sem(f"y_ready{layer}")
    z_used = mixed if layer == 0 else y_ready
    conv_done, x_done, stored = sem(f"conv_done{layer}"), sem(f"x_done{layer}"), sem(f"stored{layer}")
    mix_w, conv_w = (0, C) if layer == 0 else (None, 0)

    def block_of(pair, i):
        return pair * 2 + i

    def x_of(n):
        if layer == 0:
            return [m.x[:, k, :].rearrange("p (c j) -> p j c", j=GRID)[:, bass.ds(n * 2, 2), :] for k in range(CH)]
        return [m.x[:, k, bass.ds(n * LB, LB)] for k in range(CH)]

    with nc.Block() as block:
        @block.sync
        def _(sp):
            if w is not None:
                for k in range(kh):
                    sp.dma_start(wt[:, k, :], w[k * P:(k + 1) * P, :]).then_inc(w_in, 16)

            def pair(p):
                for i in range(2):
                    n = block_of(p, i)
                    wait_count(sp, z_used, n - 1)
                    for k in range(zh):
                        sp.dma_start(z_in[i][:, k, :], m.z_dram[k * P:(k + 1) * P, bass.ds(n * LB, LB)]).then_inc(z_loaded[i], 16)

            passes(sp, NB // 2, pair)
            if layer == 3:
                for n in range(NB):
                    sp.wait_ge(x_done, n + 1)
                    sp.dma_start(out.rearrange("(k p) n -> p k n", p=P)[:, :, n * LB:(n + 1) * LB],
                                 m.x[:, :, n * LB:(n + 1) * LB]).then_inc(stored, 16)
                sp.wait_ge(stored, 16 * NB)

        if layer != 1:
            @block.tensor
            def _(pe):
                pe.wait_ge(w_in, 16 * kh)

                def pair(p):
                    for i in range(2):
                        n = block_of(p, i)
                        if layer == 0:
                            pe.wait_ge(z_loaded[i], (p + 1) * (16 * zh))
                            wait_count(pe, y_ready, n - 1)
                            for o in range(CH):
                                for k in range(CH):
                                    mm = nc.tensor.matmul(m.psum[2 * i][:, o, :], wt[:, k, mix_w + o * P:mix_w + (o + 1) * P],
                                                          z_in[i][:, k, :], start=k == 0, stop=k == CH - 1)
                            mm.then_inc(mixed, 1)
                        pe.wait_ge(y_ready, n + 1)
                        wait_count(pe, x_done, n - 1)
                        for o in range(CH):
                            for k in range(zh):
                                mm = nc.tensor.matmul(m.psum[2 * i + 1][:, o, :], wt[:, k, conv_w + o * P:conv_w + (o + 1) * P],
                                                      y[i][:, k, :], start=k == 0, stop=k == zh - 1)
                        mm.then_inc(conv_done, 1)

                passes(pe, NB // 2, pair)

            @block.scalar
            def _(act):
                def pair(p):
                    for i in range(2):
                        n = block_of(p, i)
                        wait_count(act, conv_done, n - 1)
                        if layer == 0:
                            act.wait_ge(mixed, n + 1)
                            op = nc.scalar.activation(y[i], m.psum[2 * i][:, :, :], ACT.Copy)
                            op.then_inc(y_ready, 1)
                        else:
                            act.wait_ge(z_loaded[i], (p + 1) * (16 * zh))
                            col = {2: B_L2_V, 3: B_L3_V}[layer]
                            for k in range(zh):
                                op = nc.scalar.activation(y[i][:, k, :], z_in[i][:, k, :], ACT.Identity,
                                                          bias=m.bias[:, col + k:col + k + 1])
                            op.then_inc(y_ready, 1)

                passes(act, NB // 2, pair)

        @block.vector
        def _(dve):
            def pair(p):
                for i in range(2):
                    n = block_of(p, i)
                    if layer == 1:
                        dve.wait_ge(z_loaded[i], (p + 1) * (16 * zh))
                        wait_count(dve, x_done, n - 1)
                        for k in range(CH):
                            op = nc.vector.tensor_scalar(y[i][:, k, :], z_in[i][:, k, :], m.bias[:, B_L1_V + k:B_L1_V + k + 1],
                                                         m.bias[:, B_GAMMA:B_GAMMA + 1], ALU.add, ALU.mult)
                        op.then_inc(y_ready, 1)
                        dve.wait_ge(y_ready, n + 1)
                    else:
                        dve.wait_ge(conv_done, n + 1)
                    for k, xk in enumerate(x_of(n)):
                        if layer == 0:
                            op = nc.vector.tensor_tensor(xk, m.psum[2 * i + 1][:, k, :].rearrange("p (j c) -> p j c", j=2),
                                                         xk, ALU.add)
                        elif layer == 1:
                            op = nc.vector.tensor_tensor(xk, y[i][:, k, :], xk, ALU.add)
                        else:
                            col = {2: B_L2_O, 3: B_L3_O}[layer] + k
                            op = nc.vector.scalar_tensor_tensor(out=xk, in0=m.psum[2 * i + 1][:, k, :],
                                                                scalar=m.bias[:, col:col + 1], in1=xk,
                                                                op0=ALU.add, op1=ALU.add)
                    op.then_inc(x_done, 1)

            passes(dve, NB // 2, pair)


def build(nc, x, bias, const, proj0, proj1, proj2, proj3, fin0, fin2, fin3, out):
    with ExitStack() as ctx:
        m = Memory(nc, ctx)
        held = []

        def sem(name):
            held.append(nc.alloc_semaphore(name=name))
            return held[-1]

        load_phase(nc, sem, m, x, bias, const)
        for layer, (proj, fin) in enumerate(((proj0, fin0), (proj1, None), (proj2, fin2), (proj3, fin3))):
            project_phase(nc, sem, m, layer, proj)
            attention_phase(nc, sem, m, layer)
            finish_phase(nc, sem, m, layer, fin, out)
            nc.clear_and_free_semaphores(held)
            nc.all_engine_barrier()
            held.clear()


def _bias_table(np, i):
    table = np.zeros((P, B_COLS), np.float32)
    table[0:32, B_L1_QK] = i["L1_conv_bk"]
    table[32:64, B_L1_QK] = i["L1_conv_bq"]
    table[:, B_GAMMA] = i["L1_conv_gamma"][0]
    for col, name in ((B_L1_V, "L1_conv_bv"), (B_L2_Q, "L2_conv_bq"), (B_L2_K, "L2_conv_bk"), (B_L2_V, "L2_conv_bv"),
                      (B_L2_O, "L2_conv_bo"), (B_L3_O, "L3_conv_W_b")):
        table[:, col:col + 2] = i[name].reshape(2, P).T
    for col, name in ((B_L3_Q, "L3_conv_theta_b"), (B_L3_K, "L3_conv_phi_b"), (B_L3_V, "L3_conv_g_b")):
        table[:, col] = i[name]
    return table


def _const_table(np):
    eye = np.eye(P, dtype=np.float32)
    sum32 = np.tile(np.eye(32, dtype=np.float32), (4, 1))
    sum64 = np.tile(np.eye(64, dtype=np.float32), (2, 1))
    return np.concatenate([eye, np.ones((P, P), np.float32), sum32, sum64], axis=1)


def kernel(**inputs):
    import numpy as np
    import concourse.bacc as bacc
    from concourse.bass_utils import run_bass_kernel_spmd

    i = {k: np.asarray(v) for k, v in inputs.items()}

    def side_by_side(*names):
        return np.ascontiguousarray(np.concatenate([i[n].T for n in names], axis=1))

    arrays = {
        "x": np.ascontiguousarray(i["x"].reshape(C, T)),
        "bias": _bias_table(np, i),
        "const": _const_table(np),
        "proj0": side_by_side("L0_conv_Wf", "L0_conv_Wg", "L0_conv_Wh"),
        "proj1": side_by_side("L1_conv_wk", "L1_conv_wq", "L1_conv_wv"),
        "proj2": side_by_side("L2_conv_Wq", "L2_conv_Wk", "L2_conv_Wv"),
        "proj3": side_by_side("L3_conv_theta_w", "L3_conv_phi_w", "L3_conv_g_w"),
        "fin0": side_by_side("L0_conv_Wm", "L0_conv_Wv"),
        "fin2": side_by_side("L2_conv_Wo"),
        "fin3": side_by_side("L3_conv_W_w"),
    }
    nc = bacc.Bacc("TRN2", target_bir_lowering=False, num_devices=1)
    args = {n: nc.dram_tensor(f"in_{n}", a.shape, F32, kind="ExternalInput").ap() for n, a in arrays.items()}
    out = nc.dram_tensor("out_x", (C, T), F32, kind="ExternalOutput").ap()
    build(nc, out=out, **args)
    r = run_bass_kernel_spmd(nc, [{f"in_{n}": a for n, a in arrays.items()}], core_ids=[0])
    return r.results[0]["out_x"].reshape(1, C, 64, 64)
```

```python
import concourse.bass as bass
from concourse import mybir
from contextlib import ExitStack

F32 = mybir.dt.float32
F32R = mybir.dt.float32r
ALU = mybir.AluOpType
ACT = mybir.ActivationFunctionType
AX = mybir.AxisListType

C, T, P = 256, 4096, 128
CH = C // P
LB = 512
NB = T // LB
NC = T // P
GRID = 16
RING = 8
SPLIT_RING = 4

STACK32 = dict(q_parts=((0, 0, 0), (0, 32, 1), (0, 64, 0)), k_parts=((0, 0, 0), (0, 32, 0), (0, 64, 1)),
               products=((0, 0, 96),), shift=(0, 96), shift_product=0, k_slots=1, q_slots=1)
STACK64 = dict(q_parts=((0, 0, 0), (0, 64, 1), (1, 0, 0)), k_parts=((0, 0, 0), (0, 64, 0), (1, 0, 1)),
               products=((0, 0, 128), (1, 1, 64)), shift=(1, 64), shift_product=1, k_slots=2, q_slots=2)
STACK128 = dict(q_parts=((0, 0, 0), (1, 0, 1)), k_parts=((0, 0, 0), (1, 0, 1)),
                products=((0, 0, 128), (0, 1, 128), (1, 0, 128)), shift=(2, 0), shift_product=None,
                k_slots=2, q_slots=2)
PE_GROUPS = (2, 6)
NOT_PE = tuple(c for c in range(NC) if c // 4 not in PE_GROUPS and c % 4 != 2)
EVEN = tuple(range(0, NC, 2))
NOT_FOURTH = tuple(c for c in range(NC) if c % 4 != 3)
LAYERS = (
    dict(heads=8, dq=32, dv=32, scale=32 ** -0.5, split_v=False, pe_groups=PE_GROUPS, pool_chunks=NOT_PE, **STACK32),
    dict(heads=1, dq=32, dv=256, scale=1.0, split_v=True, pe_groups=(), pool_chunks=NOT_FOURTH, **STACK32),
    dict(heads=4, dq=64, dv=64, scale=64 ** -0.5, split_v=False, pe_groups=(), pool_chunks=EVEN, **STACK64),
    dict(heads=1, dq=128, dv=128, scale=1.0, split_v=True, pe_groups=(), pool_chunks=NOT_FOURTH, **STACK128),
)

B_L1_QK, B_L1_V, B_GAMMA, B_L2_Q, B_L2_K, B_L2_V, B_L2_O = 0, 1, 3, 4, 6, 8, 10
B_L3_Q, B_L3_K, B_L3_V, B_L3_O, B_ZERO, B_COLS = 12, 13, 14, 15, 17, 18
K_IDENT, K_ONES, K_SUM32, K_SUM64, K_COLS = 0, P, 2 * P, 2 * P + 32, 2 * P + 96
K_HEADS = {8: K_COLS, 4: K_COLS + C, 1: K_COLS + 2 * C}


def wait_count(eng, sem, value):
    if isinstance(value, int) and value <= 0:
        return
    eng.wait_ge(sem, value)


class Memory:

    def __init__(self, nc, ctx):
        def sb(name, shape, dt=F32):
            return ctx.enter_context(nc.sbuf_tensor(name, shape, dt))

        self.x = sb("x", [P, CH, T])
        self.qk = sb("qk", [P, 27 * 1024], F32R)
        self.v = sb("v", [P, 8192])
        self.probs = sb("probs", [P, RING, LB])
        self.sums = sb("sums", [P, 2, 2, LB])
        self.total = sb("total", [P, LB])
        self.z = sb("z", [P, 2, LB])
        self.folded = sb("folded", [P, LB])
        self.bias = sb("bias", [P, B_COLS])
        self.const = sb("const", [P, K_COLS])
        self.rowmax = sb("rowmax", [P, 4, NB])
        self.negmax = sb("negmax", [P, 4])
        self.shift = sb("shift", [P, 4, 2])
        self.ones2 = sb("ones2", [2, P], F32R)
        self.psum = [ctx.enter_context(nc.psum_tensor(f"bank{i}", [P, 2, LB], F32)) for i in range(4)]

        def dram(name, shape, dt):
            return nc.dram_tensor(name, shape, dt, kind="Internal").ap()

        self.q_dram = dram("q_dram", (2, C, T), F32)
        self.k_dram = dram("k_dram", (2, C, T), F32)
        self.v_dram = dram("v_dram", (2, T, C), F32)
        self.z_dram = dram("z_dram", (C, T), F32)
        self.den_dram = dram("den_dram", (8 * T,), F32)
        self.recip_dram = dram("recip_dram", (2 * 8 * T,), F32)

    def bank(self, i):
        return self.psum[i // 2][:, i % 2, :]


def load_phase(nc, sem, m, x, bias, const):
    loaded = sem("inputs_loaded")
    with nc.Block() as block:
        @block.sync
        def _(sp):
            for half in range(CH):
                sp.dma_start(m.x[:, half, :], x[half * P:(half + 1) * P, :]).then_inc(loaded, 16)
            sp.dma_start(m.bias[:, :], bias).then_inc(loaded, 16)
            sp.dma_start(m.const[:, :], const[:, 0:K_COLS]).then_inc(loaded, 16)
            sp.wait_ge(loaded, 64)


def weights_view(m, cols):
    return m.probs[:, :, :].rearrange("p a b -> p (a b)")[:, 0:CH * cols].rearrange("p (k n) -> p k n", k=CH)


def passes(eng, trips, body):
    body(0)
    if trips > 1:
        with eng.Fori(1, trips) as trip:
            body(trip)


def project_phase(nc, sem, m, layer, w):
    cfg = LAYERS[layer]
    cols = w.shape[1]
    wt = weights_view(m, cols)
    hi = [m.qk[:, s * LB:(s + 1) * LB] for s in range(4)]
    lo = [m.qk[:, (4 + s) * LB:(5 + s) * LB] for s in range(4)]
    vs, vs_lo = [[m.v[:, (first + s) * LB:(first + s + 1) * LB] for s in range(4)] for first in (0, 4)]
    w_loaded = sem(f"w_loaded{layer}")
    qk_done, hi_done, lo_done = sem(f"qk_done{layer}"), sem(f"hi_done{layer}"), sem(f"lo_done{layer}")
    v_done, v_copied, v_hi_done = sem(f"v_done{layer}"), sem(f"v_copied{layer}"), sem(f"v_hi_done{layer}")
    qk_stored = [sem(f"qk_stored{layer}_{s}") for s in range(4)]
    v_stored = [sem(f"v_stored{layer}_{s}") for s in range(4)]

    groups, rows = ((2, P), (1, 64), (4, P), (2, P))[layer]
    trips, body = ((1, 32), (2, 4), (4, 8), (4, 4))[layer]
    trip_px = body // groups * LB
    stores = (4, 4, 2, 2)[layer]
    v_trips, v_body = (4, 4) if layer == 0 else (1, NC)
    v_parts = 2 if cfg["split_v"] else 1
    v_col = (2 * C, 64, 2 * C, C)[layer]
    v_n = LB if layer == 0 else cfg["heads"] * cfg["dv"]

    def bias_of(i):
        col = (B_ZERO, B_L1_QK, B_L2_Q + i % groups, B_L3_Q + i % groups)[layer]
        return m.bias[0:rows, col:col + 1]

    with nc.Block() as block:
        @block.tensor
        def _(pe):
            pe.wait_ge(w_loaded, 16 * CH)

            def qk_tiles(trip):
                for i in range(body):
                    wait_count(pe, lo_done, trip * body + i - 3)
                    for k in range(CH):
                        if layer == 0:
                            lhs, rhs = m.x[:, k, i * P:(i + 1) * P], wt[:, k, 0:LB]
                        else:
                            lhs = wt[:, k, i % groups * rows:(i % groups + 1) * rows]
                            rhs = m.x[:, k, bass.ds(trip * trip_px + i // groups * LB, LB)]
                        mm = nc.tensor.matmul(m.bank(i % 4)[0:rows, :], lhs, rhs, start=k == 0, stop=k == CH - 1)
                    mm.then_inc(qk_done, 1)

            def v_tiles(trip):
                for i in range(v_body):
                    wait_count(pe, v_copied, trip * v_body + i - 3)
                    for k in range(CH):
                        if layer == 0:
                            lhs = wt[:, k, v_col + i % CH * P:v_col + (i % CH + 1) * P]
                            rhs = m.x[:, k, bass.ds(trip * (2 * LB) + i // CH * LB, LB)]
                        else:
                            lhs, rhs = m.x[:, k, i * P:(i + 1) * P], wt[:, k, v_col:v_col + v_n]
                        mm = nc.tensor.matmul(m.bank(4 + i % 4)[:, 0:v_n], lhs, rhs, start=k == 0, stop=k == CH - 1)
                    mm.then_inc(v_done, 1)

            passes(pe, trips, qk_tiles)
            passes(pe, v_trips, v_tiles)

        @block.scalar
        def _(act):
            def round_hi(trip):
                for i in range(body):
                    act.wait_ge(qk_done, trip * body + i + 1)
                    wait_count(act, qk_stored[i % 4], (trip * (body // 4) + i // 4) * (16 * stores))
                    nc.scalar.activation(hi[i % 4][0:rows, :], m.bank(i % 4)[0:rows, :], ACT.Identity,
                                         bias=bias_of(i)).then_inc(hi_done, 1)

            def round_v(trip):
                for i in range(v_body):
                    act.wait_ge(v_done, trip * v_body + i + 1)
                    wait_count(act, v_stored[i % 4], (trip * (v_body // 4) + i // 4) * (16 * v_parts))
                    nc.scalar.activation(vs[i % 4][:, 0:v_n].bitcast(F32R), m.bank(4 + i % 4)[:, 0:v_n],
                                         ACT.Copy).then_inc(v_hi_done, 1)

            passes(act, trips, round_hi)
            if cfg["split_v"]:
                passes(act, v_trips, round_v)

        @block.vector
        def _(dve):
            def round_lo(trip):
                for i in range(body):
                    dve.wait_ge(hi_done, trip * body + i + 1)
                    nc.vector.scalar_tensor_tensor(out=lo[i % 4][0:rows, :], in0=m.bank(i % 4)[0:rows, :],
                                                   scalar=bias_of(i), in1=hi[i % 4][0:rows, :],
                                                   op0=ALU.add, op1=ALU.subtract).then_inc(lo_done, 1)

            def copy_v(trip):
                for i in range(v_body):
                    bank = m.bank(4 + i % 4)[:, 0:v_n]
                    if cfg["split_v"]:
                        dve.wait_ge(v_hi_done, trip * v_body + i + 1)
                        nc.vector.tensor_tensor(vs_lo[i % 4][:, 0:v_n].bitcast(F32R), bank, vs[i % 4][:, 0:v_n],
                                                ALU.subtract).then_inc(v_copied, 1)
                        continue
                    dve.wait_ge(v_done, trip * v_body + i + 1)
                    wait_count(dve, v_stored[i % 4], (trip * (v_body // 4) + i // 4) * 16)
                    nc.vector.tensor_copy(vs[i % 4][:, 0:v_n], bank).then_inc(v_copied, 1)

            passes(dve, trips, round_lo)
            passes(dve, v_trips, copy_v)

        @block.sync
        def _(sp):
            for k in range(CH):
                sp.dma_start(wt[:, k, :], w[k * P:(k + 1) * P, :]).then_inc(w_loaded, 16)

            def store_qk(trip):
                for i in range(body):
                    sp.wait_ge(lo_done, trip * body + i + 1)
                    for part, tile in enumerate((hi[i % 4], lo[i % 4])):
                        if layer == 0:
                            at = (slice(i % 2 * P, (i % 2 + 1) * P), slice(i // 2 * C, (i // 2 + 1) * C))
                            moves = ((m.q_dram[part][at], tile[:, 0:C]), (m.k_dram[part][at], tile[:, C:2 * C]))
                        else:
                            px = bass.ds(trip * trip_px + i // groups * LB, LB)
                            if layer == 1:
                                moves = ((m.q_dram[part, 0:32, px], tile[0:32, :]), (m.k_dram[part, 0:32, px], tile[32:64, :]))
                            else:
                                g = i % groups
                                half = g % (groups // 2) * P
                                to = m.q_dram if g < groups // 2 else m.k_dram
                                moves = ((to[part, half:half + P, px], tile[:, :]),)
                        for dst, src in moves:
                            sp.dma_start(dst, src.bitcast(F32)).then_inc(qk_stored[i % 4], 16)

            v_tokens = m.v_dram[0].rearrange("(j h p) n -> h p j n", h=CH, p=P)

            def store_v(trip):
                for i in range(v_body):
                    sp.wait_ge(v_copied, trip * v_body + i + 1)
                    if layer == 0:
                        dst = v_tokens[i % CH][:, bass.ds(trip * 4 + i // CH * 2, 2), :]
                        src = vs[i % 4].rearrange("p (j n) -> p j n", j=2)
                    else:
                        dst, src = m.v_dram[0, i * P:(i + 1) * P, 0:v_n], vs[i % 4][:, 0:v_n]
                    sp.dma_start(dst, src).then_inc(v_stored[i % 4], 16)
                    if cfg["split_v"]:
                        sp.dma_start(m.v_dram[1, i * P:(i + 1) * P, 0:v_n], vs_lo[i % 4][:, 0:v_n]).then_inc(v_stored[i % 4], 16)

            passes(sp, trips, store_qk)
            passes(sp, v_trips, store_v)
            for s in range(4):
                sp.wait_ge(qk_stored[s], trips * (body // 4) * 16 * stores)
                sp.wait_ge(v_stored[s], v_trips * (v_body // 4) * 16 * v_parts)


def attention_phase(nc, sem, m, layer):
    cfg = LAYERS[layer]
    H, dq, dv, products = cfg["heads"], cfg["dq"], cfg["dv"], cfg["products"]
    ks, qs = cfg["k_slots"], cfg["q_slots"]
    U = H * NB
    NT, per_row = 4 * T // LB, T // LB
    accs = -(-dv // P)
    width = min(dv, P)
    col_tiles = P // width
    shift_slot, shift_row = cfg["shift"]
    b_slots = max(qs, shift_slot + 1)
    stores = 16 * (accs + 1)
    n_q, n_k = len(cfg["q_parts"]), len(cfg["k_parts"])
    split = cfg["split_v"]
    v_parts = 2 if split else 1
    pool_chunks = cfg["pool_chunks"]
    pe_groups = cfg["pe_groups"]
    vec_chunks = tuple(c for c in range(NC) if c not in pool_chunks and c // 4 not in pe_groups)
    n_pool, n_vec = len(pool_chunks) - 1, max(len(vec_chunks) - 1, 0)
    group = col_tiles
    groups = NC // group
    FOLD_TILE, FOLD_AT, ADD_AT, PE_SUM_AT = 16, (16 * 29 // 32), 7, 4
    fold_rows = 2 * width if col_tiles > 1 else 1
    VALUES_AT = {1: 0, 2: 1, 4: 1}[group]
    copy_at = {1: 0, 2: 2, 4: 2}[group]
    fold_bank, shift_bank = m.bank(FOLD_TILE % 3), m.bank(2)
    SHIFT_AT = NC - 2
    tiles_at = [[k for k in range(NT) if k * 29 // NT == c] for c in range(NC)]
    vec_at = [[j for j in range(n_vec) if min(vec_chunks[j + 1] + 2, NC - 1) == c] for c in range(NC)]

    at = 0

    def take(n):
        nonlocal at
        at += n
        return m.qk[:, at - n:at]

    k_still = take(ks * T).rearrange("p (s n) -> p s n", s=ks)
    k_move = take(2 * ks * T) if H > 1 else None
    q_still = take(qs * LB).rearrange("p (s n) -> p s n", s=qs)
    q_move = take(2 * b_slots * LB)
    if split:
        v_head, v_lo = [take(NC * dv).rearrange("p (c d) -> p c d", c=NC) for _ in range(2)]
        probs_hi, probs_lo = [take(SPLIT_RING * LB).rearrange("p (r n) -> p r n", r=SPLIT_RING) for _ in range(2)]
    else:
        v_head = m.v[:, 0:NC * dv].rearrange("p (c d) -> p c d", c=NC)
    rounded = m.shift[:, :, :].bitcast(F32R)

    def score_bank(c):
        return m.bank(3 + c % 3)

    def sum_step(chunks, engine, j):
        early, whole = m.sums[:, engine, 0, :], m.sums[:, engine, 1, :]
        n_early = len([c for c in chunks[1:] if c < FOLD_AT])
        before = m.probs[:, chunks[0] % RING, :] if j == 0 else early if j <= n_early else whole
        return early if j < n_early else whole, before, m.probs[:, chunks[j + 1] % RING, :]

    def moving_q(u, slot, r0, r1):
        return q_move[r0:r1, bass.ds(u % 2 * (b_slots * LB) + slot * LB, LB)]

    def moving_k(b, slot, rows, col):
        if H == 1:
            return k_still[0:rows, slot, col:col + LB]
        return k_move[0:rows, bass.ds(b // NB % 2 * (ks * T) + slot * T + col, LB)]

    def max_bank(k):
        return m.bank((k if k < FOLD_TILE else k + 1) % 3)

    pe_sum_copy = m.z[:, 1, :]
    pe_sum = m.bank(7)
    acc = [m.bank(6), m.bank(7)][0:accs]

    s = {n: sem(f"{n}{layer}") for n in (
        "ones_ready", "max_ready", "max_taken", "max_chained", "shift_ready", "shift_moved", "shift_copied",
        "scores_ready", "probs_ready", "lo_ready", "values_done", "values_copied", "pe_summed", "sum_copied", "pool_summed", "vec_summed",
        "pe_sum_added", "totals", "den_ready", "den_copied", "z_stored", "k_moving_in", "q_moving_in")}
    q_still_in = [sem(f"q_still_in{layer}_{t}") for t in range(4)]
    k_still_in = [sem(f"k_still_in{layer}_{t}") for t in range(4)]
    v_in = [sem(f"v_in{layer}_{t}") for t in range(4)]

    def units(eng, unit):
        unit(0, True, False)
        with eng.Fori(1, U - 1) as u:
            unit(u, False, False)
        unit(U - 1, False, True)

    with nc.Block() as block:
        @block.tensor
        def _(pe):
            def max_tile(b, k):
                t, part = k // per_row, k % per_row
                if k == 0:
                    if H > 1:
                        pe.wait_ge(s["k_moving_in"], (b // NB + 1) * (16 * n_k))
                    elif isinstance(b, int) and b == 0:
                        for piece in range(4):
                            pe.wait_ge(k_still_in[piece], 16 * n_k)
                if part == 0:
                    pe.wait_ge(q_still_in[t], (b + 1) * (16 * n_q))
                if k == FOLD_TILE + 2:
                    wait_count(pe, s["den_copied"], b - 1)
                else:
                    wait_count(pe, s["max_taken"], b * NT + k - (1 if k in (FOLD_TILE, FOLD_TILE + 1) else 2))
                for i, (sk, sq, rows) in enumerate(products):
                    mm = nc.tensor.matmul(max_bank(k), q_still[0:rows, sq, t * P:(t + 1) * P],
                                          moving_k(b, sk, rows, part * LB), start=i == 0, stop=i == len(products) - 1)
                mm.then_inc(s["max_ready"], 1)

            def shift_rows(b):
                pe.wait_ge(s["shift_ready"], b + 1)
                for t in range(4):
                    mm = nc.tensor.matmul(shift_bank[0:2, t * P:(t + 1) * P], m.shift[:, t, :],
                                          m.const[:, K_IDENT:K_IDENT + P], start=True, stop=True)
                mm.then_inc(s["shift_moved"], 1)

            def scores(u, c):
                if c == 0:
                    pe.wait_ge(s["shift_copied"], u + 1)
                    pe.wait_ge(s["q_moving_in"], (u + 1) * (16 * n_q))
                if c % 8 == 0:
                    pe.wait_ge(k_still_in[c // 8], (u // NB + 1) * (16 * n_k))
                wait_count(pe, s["probs_ready"], u * NC + (c - 1 if c < 2 else 0 if c == 2 else c - 2))
                out = score_bank(c)
                for i, (sk, sq, rows) in enumerate(products):
                    rows += 2 * (i == cfg["shift_product"])
                    last = i == len(products) - 1 and cfg["shift_product"] is not None
                    mm = nc.tensor.matmul(out, k_still[0:rows, sk, c * P:(c + 1) * P], moving_q(u, sq, 0, rows),
                                          start=i == 0, stop=last)
                if cfg["shift_product"] is None:
                    mm = nc.tensor.matmul(out, m.ones2[:, :], moving_q(u, shift_slot, 0, 2), start=False, stop=True)
                mm.then_inc(s["scores_ready"], 1)

            def values(u, g):
                pe.wait_ge(s["probs_ready"], u * NC + group * (g + 1))
                if g == 0:
                    wait_count(pe, s["values_copied"], u)
                if g * group % 8 == 0:
                    pe.wait_ge(v_in[g * group // 8], (u // NB + 1) * (16 * v_parts))
                if split:
                    for last, (v, p) in enumerate(((v_head, probs_hi), (v_lo, probs_hi), (v_head, probs_lo))):
                        if last == 2:
                            pe.wait_ge(s["lo_ready"], u * NC + g + 1)
                        for a in range(accs):
                            mm = nc.tensor.matmul(acc[a], v[:, g, a * P:(a + 1) * P], p[:, g % SPLIT_RING, :],
                                                  start=g == 0 and last == 0, stop=g == NC - 1 and last == 2)
                    mm.then_inc(s["values_done"], 1)
                    return
                for c in range(group * g, group * (g + 1)):
                    r = c % group * width
                    for a in range(accs):
                        mm = nc.tensor.matmul(acc[a][r:r + width, :], v_head[:, c, a * P:a * P + width],
                                              m.probs[:, c % RING, :], start=c < group, stop=c >= NC - group)
                mm.then_inc(s["values_done"], 1)

            def sum_probs(u, g):
                if g == pe_groups[0]:
                    wait_count(pe, s["sum_copied"], u)
                for c in range(group * g, group * (g + 1)):
                    r = c % group * width
                    mm = nc.tensor.matmul(pe_sum[r:r + width, :], m.const[:, K_SUM32:K_SUM32 + width],
                                          m.probs[:, c % RING, :], start=g == pe_groups[0], stop=g == pe_groups[-1])
                mm.then_inc(s["pe_summed"], 1)

            def denominators(u):
                pe.wait_ge(s["totals"], u + 1)
                pe.wait_ge(s["values_copied"], u + 1)
                if not (isinstance(u, int) and u >= U - 2):
                    pe.wait_ge(s["max_taken"], (u + 2) * NT + FOLD_TILE - 2)
                n_ones = width if col_tiles > 1 else 1
                mm = nc.tensor.matmul(fold_bank[0:n_ones, :], m.const[:, K_ONES:K_ONES + n_ones], m.total[:, :],
                                      start=True, stop=True)
                if col_tiles > 1:
                    k = K_SUM32 if width == 32 else K_SUM64
                    mm = nc.tensor.matmul(fold_bank[width:2 * width, :], m.const[:, k:k + width], m.z[:, 0, :],
                                          start=True, stop=True)
                mm.then_inc(s["den_ready"], 1)

            def unit(u, first, last):
                for c in range(NC):
                    if c > 0:
                        scores(u, c)
                    if not last:
                        for k in tiles_at[c]:
                            if k == FOLD_TILE and not first:
                                denominators(u - 1)
                            max_tile(u + 1, k)
                    elif c == FOLD_AT:
                        denominators(u - 1)
                    if c == 0:
                        scores(u, c)
                    if c == SHIFT_AT and not last:
                        shift_rows(u + 1)
                    g = c // group
                    if c % group == VALUES_AT:
                        if g > 0:
                            values(u, g - 1)
                        elif not first:
                            values(u - 1, groups - 1)
                    if pe_groups and c % group == group - 1:
                        if g > 0 and g - 1 in pe_groups:
                            sum_probs(u, g - 1)
                        if g == 0 and groups - 1 in pe_groups and not first:
                            sum_probs(u - 1, groups - 1)

            pe.wait_ge(s["ones_ready"], 1)
            for k in range(NT):
                max_tile(0, k)
            shift_rows(0)
            units(pe, unit)
            values(U - 1, groups - 1)
            if groups - 1 in pe_groups:
                sum_probs(U - 1, groups - 1)
            denominators(U - 1)

        @block.scalar
        def _(act):
            def copy_shift(u):
                act.wait_ge(s["shift_moved"], u + 1)
                nc.scalar.activation(moving_q(u, shift_slot, shift_row, shift_row + 2), shift_bank[0:2, :],
                                     ACT.Copy).then_inc(s["shift_copied"], 1)

            def free_probs(u, c):
                if c % group == 0:
                    wait_count(act, s["values_done"], u * groups + (c - (SPLIT_RING if split else RING)) // group + 1)
                before = c - RING
                uu = u if before >= 0 else u - 1
                before %= NC
                if before in pool_chunks:
                    wait_count(act, s["pool_summed"], uu * n_pool + max(pool_chunks.index(before), 1))
                elif before // 4 in pe_groups:
                    wait_count(act, s["pe_summed"], uu * len(pe_groups) + pe_groups.index(before // 4) + 1)
                else:
                    wait_count(act, s["vec_summed"], uu * n_vec + max(vec_chunks.index(before), 1))

            def copy_values(u):
                act.wait_ge(s["values_done"], (u + 1) * groups)
                if col_tiles == 1:
                    wait_count(act, s["z_stored"], u * stores)
                for a in range(accs):
                    op = nc.scalar.activation(m.z[:, a, :], acc[a], ACT.Copy)
                op.then_inc(s["values_copied"], 1)

            def copy_sum(u):
                act.wait_ge(s["pe_summed"], (u + 1) * len(pe_groups))
                wait_count(act, s["pe_sum_added"], u)
                nc.scalar.activation(pe_sum_copy, pe_sum, ACT.Copy).then_inc(s["sum_copied"], 1)

            def copy_denominators(u):
                act.wait_ge(s["den_ready"], u + 1)
                wait_count(act, s["z_stored"], u * stores)
                nc.scalar.activation(m.folded[0:fold_rows, :], fold_bank[0:fold_rows, :],
                                     ACT.Copy).then_inc(s["den_copied"], 1)

            def unit(u, first, last):
                for c in range(NC):
                    act.wait_ge(s["scores_ready"], u * NC + c + 1)
                    free_probs(u, c)
                    if split:
                        nc.scalar.activation(probs_hi[:, c % SPLIT_RING, :], score_bank(c), ACT.Exp, scale=cfg["scale"])
                    nc.scalar.activation(m.probs[:, c % RING, :], score_bank(c), ACT.Exp,
                                         scale=cfg["scale"]).then_inc(s["probs_ready"], 1)
                    if c == copy_at and not first:
                        copy_values(u - 1)
                    if c == PE_SUM_AT and pe_groups and not first:
                        copy_sum(u - 1)
                    if c == FOLD_AT and not first:
                        copy_denominators(u - 1)
                    if c == SHIFT_AT and not last:
                        copy_shift(u + 1)

            copy_shift(0)
            units(act, unit)
            copy_values(U - 1)
            if pe_groups:
                copy_sum(U - 1)
            copy_denominators(U - 1)

        @block.vector
        def _(dve):
            def take_max(b, k):
                dve.wait_ge(s["max_ready"], b * NT + k + 1)
                if k == 0:
                    wait_count(dve, s["shift_ready"], b)
                nc.vector.reduce_max(m.rowmax[:, k // per_row, k % per_row:k % per_row + 1], max_bank(k),
                                     AX.X).then_inc(s["max_taken"], 1)

            def make_shift(b):
                dve.wait_ge(s["max_taken"], (b + 1) * NT)
                nc.vector.reduce_max(m.negmax[:, :], m.rowmax[:, :, :], AX.X).then_inc(s["max_chained"], 1)
                dve.wait_ge(s["max_chained"], b * 2 + 1)
                wait_count(dve, s["shift_moved"], b)
                nc.vector.tensor_scalar(rounded[:, :, 0], m.negmax[:, :], -1.0, None,
                                        ALU.mult).then_inc(s["max_chained"], 1)
                dve.wait_ge(s["max_chained"], b * 2 + 2)
                nc.vector.scalar_tensor_tensor(out=rounded[:, :, 1], in0=m.negmax[:, :], scalar=-1.0,
                                               in1=m.shift[:, :, 0], op0=ALU.mult,
                                               op1=ALU.subtract).then_inc(s["shift_ready"], 1)

            def add(u, j):
                out, before, tile_in = sum_step(vec_chunks, 1, j)
                dve.wait_ge(s["probs_ready"], u * NC + vec_chunks[j + 1] + 1)
                wait_count(dve, s["vec_summed"], u * n_vec + j)
                wait_count(dve, s["totals"], u if vec_chunks[j + 1] >= FOLD_AT else 0)
                nc.vector.tensor_tensor(out, before, tile_in, ALU.add).then_inc(s["vec_summed"], 1)

            def add_pe_sum(u):
                dve.wait_ge(s["sum_copied"], u + 1)
                dve.wait_ge(s["vec_summed"], (u + 1) * n_vec)
                whole = m.sums[:, 1, 1, :]
                nc.vector.tensor_tensor(whole, whole, pe_sum_copy, ALU.add).then_inc(s["pe_sum_added"], 1)

            def split_probs(u, c):
                dve.wait_ge(s["probs_ready"], u * NC + c + 1)
                wait_count(dve, s["values_done"], u * NC + c - SPLIT_RING + 1)
                nc.vector.tensor_tensor(probs_lo[:, c % SPLIT_RING, :], m.probs[:, c % RING, :],
                                        probs_hi[:, c % SPLIT_RING, :], ALU.subtract).then_inc(s["lo_ready"], 1)

            def unit(u, first, last):
                for c in range(NC):
                    if not last:
                        for k in tiles_at[c]:
                            take_max(u + 1, k)
                            if k == NT - 1:
                                make_shift(u + 1)
                    if split:
                        split_probs(u, c)
                    for j in vec_at[c]:
                        add(u, j)
                    if c == PE_SUM_AT + 1 and pe_groups and not first:
                        add_pe_sum(u - 1)

            for k in range(NT):
                take_max(0, k)
            make_shift(0)
            units(dve, unit)
            if pe_groups:
                add_pe_sum(U - 1)

        @block.gpsimd
        def _(pool):
            if cfg["shift_product"] is None:
                nc.gpsimd.memset(m.ones2[:, :].bitcast(F32), 1.0).then_inc(s["ones_ready"], 1)
            else:
                nc.gpsimd.memset(k_still[shift_row:shift_row + 2, shift_slot, :].bitcast(F32), 1.0).then_inc(s["ones_ready"], 1)

            def add(u, j):
                out, before, tile_in = sum_step(pool_chunks, 0, j)
                pool.wait_ge(s["probs_ready"], u * NC + pool_chunks[j + 1] + 1)
                wait_count(pool, s["pool_summed"], u * n_pool + j)
                if pool_chunks[j + 1] >= FOLD_AT:
                    wait_count(pool, s["totals"], u)
                nc.gpsimd.tensor_tensor(out, before, tile_in, ALU.add).then_inc(s["pool_summed"], 1)

            def add_engines(u):
                pool.wait_ge(s["pool_summed"], (u + 1) * n_pool)
                if pe_groups:
                    pool.wait_ge(s["pe_sum_added"], u + 1)
                else:
                    pool.wait_ge(s["vec_summed"], (u + 1) * n_vec)
                wait_count(pool, s["den_ready"], u)
                nc.gpsimd.tensor_tensor(m.total[:, :], m.sums[:, 0, 1, :], m.sums[:, 1, 1, :],
                                        ALU.add).then_inc(s["totals"], 1)

            def unit(u, first, last):
                for j in range(n_pool):
                    if not first and pool_chunks[j] <= ADD_AT < pool_chunks[j + 1]:
                        add_engines(u - 1)
                    add(u, j)

            units(pool, unit)
            add_engines(U - 1)

        @block.sync
        def _(sp):
            def load_q(dst, part, b, first_token, n, done):
                sp.dma_start(dst.bitcast(F32), m.q_dram[part, bass.ds(b // NB * dq, dq),
                                           bass.ds(b % NB * LB + first_token, n)]).then_inc(done, 16)

            def load_q_still(b, t):
                wait_count(sp, s["max_ready"], (b - 1) * NT + (t + 1) * per_row)
                for slot, r, part in cfg["q_parts"]:
                    load_q(q_still[r:r + dq, slot, t * P:(t + 1) * P], part, b, t * P, P, q_still_in[t])

            def load_q_moving(b):
                wait_count(sp, s["scores_ready"], (b - 1) * NC + 1)
                for slot, r, part in cfg["q_parts"]:
                    load_q(moving_q(b, slot, r, r + dq), part, b, 0, LB, s["q_moving_in"])

            def load_k_moving(h):
                wait_count(sp, s["max_ready"], (h - 1) * (NB * NT) + 1)
                for slot, r, part in cfg["k_parts"]:
                    sp.dma_start(k_move[r:r + dq, bass.ds(h % 2 * (ks * T) + slot * T, T)].bitcast(F32),
                                 m.k_dram[part, bass.ds(h * dq, dq), :]).then_inc(s["k_moving_in"], 16)

            def load_piece(h, t):
                wait_count(sp, s["values_done"], h * (NB * groups) + ((t + 1) * (groups // 4) - groups))
                for slot, r, part in cfg["k_parts"]:
                    sp.dma_start(k_still[r:r + dq, slot, t * 8 * P:(t + 1) * 8 * P].bitcast(F32),
                                 m.k_dram[part, bass.ds(h * dq, dq), t * 8 * P:(t + 1) * 8 * P]).then_inc(k_still_in[t], 16)
                for part, to in enumerate((v_head, v_lo) if split else (v_head,)):
                    src = m.v_dram[part].rearrange("(c p) d -> p c d", p=P)[:, t * 8:(t + 1) * 8, bass.ds(h * dv, dv)]
                    sp.dma_start(to[:, t * 8:(t + 1) * 8, :].bitcast(F32), src).then_inc(v_in[t], 16)

            def store_z(u):
                sp.wait_ge(s["den_copied"], u + 1)
                for a in range(accs):
                    src = m.z[:, a, :] if col_tiles == 1 else m.folded[width:2 * width, :]
                    sp.dma_start(m.z_dram[bass.ds(u // NB * dv + a * P, width), bass.ds(u % NB * LB, LB)],
                                 src).then_inc(s["z_stored"], 16)
                sp.dma_start(m.den_dram[bass.ds(u * LB, LB)].rearrange("(o n) -> o n", o=1),
                             m.folded[0:1, :]).then_inc(s["z_stored"], 16)

            def unit(u, moving, still, next_head, first=False):
                if moving:
                    load_q_moving(u + 1)
                for t in range(4):
                    if t == 2 and not first:
                        store_z(u - 1)
                    if still:
                        load_q_still(u + 2, t)
                    if next_head is not None:
                        load_piece(next_head, t)

            for t in range(4):
                load_q_still(0, t)
            if H > 1:
                load_k_moving(0)
            for t in range(4):
                load_piece(0, t)
            load_q_moving(0)
            for t in range(4):
                load_q_still(1, t)
            unit(0, True, True, None, True)
            if H > 1:
                load_k_moving(1)
                with sp.Fori(1, NB - 1) as u:
                    unit(u, True, True, None)
                unit(NB - 1, True, True, 1)
                with sp.Fori(1, H - 1) as h:
                    load_k_moving(h + 1)
                    with sp.Fori(0, NB - 1) as n:
                        unit(h * NB + n, True, True, None)
                    unit(h * NB + NB - 1, True, True, h + 1)
            with sp.Fori(max((H - 1) * NB, 1), U - 2) as u:
                unit(u, True, True, None)
            unit(U - 2, True, False, None)
            store_z(U - 2)
            store_z(U - 1)
            sp.wait_ge(s["z_stored"], U * stores)


def finish_phase(nc, sem, m, layer, w, const, out):
    H = LAYERS[layer]["heads"]
    per_row = H * T // P
    zh = 1 if layer == 3 else CH
    rh = CH if H > 1 else 1
    weights = m.probs[:, :, :].rearrange("p a b -> p (a b)")
    if w is not None:
        kh = w.shape[0] // P
        w_view = weights[:, 0:kh * w.shape[1]].rearrange("p (k n) -> p k n", k=kh)
        conv_w = w_view if layer else weights[:, kh * w.shape[1]:][:, 0:CH * C].rearrange("p (k n) -> p k n", k=CH)
    z_in = [m.v[:, i * 2 * LB:(i + 1) * 2 * LB].rearrange("p (k n) -> p k n", k=2) for i in range(2)]
    y = [m.v[:, (i + 2) * 2 * LB:(i + 3) * 2 * LB].rearrange("p (k n) -> p k n", k=2) for i in range(2)]
    packed = m.total[:, 0:per_row]
    packed_parts = m.qk[:, T:T + 2 * per_row].rearrange("p (k n) -> p k n", k=2)
    recip_rows = m.qk[0:2 * H, 0:T]
    heads_loaded = m.sums[:, :, :, :].rearrange("p a b n -> p (a b n)")[0:2 * H, 0:rh * P]
    heads_of = m.qk[0:2 * H, 2 * T:2 * T + rh * P]
    w_in, z_loaded = sem(f"fw_in{layer}"), [sem(f"z_loaded{layer}_{i}") for i in range(2)]
    heads_in, heads_copied = sem(f"heads_in{layer}"), sem(f"heads_copied{layer}")
    den_in, inverted = sem(f"den_in{layer}"), sem(f"inverted{layer}")
    recip_stored, recip_in = sem(f"recip_stored{layer}"), sem(f"recip_in{layer}")
    merged, merge_copied = sem(f"merged{layer}"), sem(f"merge_copied{layer}")
    spread, divided = sem(f"spread{layer}"), sem(f"divided{layer}")
    y_ready = sem(f"y_ready{layer}") if layer else divided
    conv_done, x_done, stored = sem(f"conv_done{layer}"), sem(f"x_done{layer}"), sem(f"stored{layer}")

    def x_of(n):
        if layer == 0:
            return [m.x[:, k, :].rearrange("p (c j) -> p j c", j=GRID)[:, bass.ds(n * 2, 2), :] for k in range(CH)]
        return [m.x[:, k, bass.ds(n * LB, LB)] for k in range(CH)]

    def blocks(eng, ahead, behind):
        def pair(p, last):
            ahead(p * 2 + 1, p, 1)
            behind(p * 2, 0)
            if not last:
                ahead(p * 2 + 2, p + 1, 0)
            behind(p * 2 + 1, 1)

        ahead(0, 0, 0)
        pair(0, False)
        with eng.Fori(1, NB // 2 - 1) as p:
            pair(p, False)
        pair(NB // 2 - 1, True)

    with nc.Block() as block:
        @block.sync
        def _(sp):
            sp.dma_start(packed, m.den_dram[0:H * T].rearrange("(p n) -> p n", p=P)).then_inc(den_in, 16)
            sp.dma_start(heads_loaded, const[0:2 * H, K_HEADS[H]:K_HEADS[H] + rh * P]).then_inc(heads_in, 16)
            if w is not None:
                for k in range(kh):
                    sp.dma_start(w_view[:, k, :], w[k * P:(k + 1) * P, :]).then_inc(w_in, 16)
            sp.wait_ge(inverted, 3)
            sp.dma_start(m.recip_dram[0:2 * H * T].rearrange("(k p n) -> p k n", k=2, p=P),
                         packed_parts.bitcast(F32)).then_inc(recip_stored, 16)
            sp.wait_ge(recip_stored, 16)
            sp.dma_start(recip_rows.bitcast(F32), m.recip_dram[0:2 * H * T].rearrange("(h n) -> h n", h=2 * H)).then_inc(recip_in, 16)
            if layer == 3:
                for n in range(NB):
                    sp.wait_ge(x_done, n + 1)
                    sp.dma_start(out.rearrange("(k p) n -> p k n", p=P)[:, :, n * LB:(n + 1) * LB],
                                 m.x[:, :, n * LB:(n + 1) * LB]).then_inc(stored, 16)
                sp.wait_ge(stored, 16 * NB)

        @block.gpsimd
        def _(pool):
            def pair(p):
                for i in range(2):
                    n = p * 2 + i
                    wait_count(pool, y_ready, n - 1)
                    for k in range(zh):
                        pool.dma_start(z_in[i][:, k, :], m.z_dram[k * P:(k + 1) * P, bass.ds(n * LB, LB)]).then_inc(z_loaded[i], 16)

            passes(pool, NB // 2, pair)

        @block.tensor
        def _(pe):
            def spread_recip(n, p, i):
                wait_count(pe, divided, n - 1)
                for k in range(rh):
                    mm = nc.tensor.matmul(m.psum[2 * i][:, k, :], heads_of[:, k * P:(k + 1) * P],
                                          recip_rows[:, bass.ds(n * LB, LB)], start=True, stop=True)
                mm.then_inc(spread, 1)

            def conv(n, i):
                if layer == 1:
                    return
                pe.wait_ge(y_ready, n + 1)
                wait_count(pe, x_done, n - 1)
                for o in range(CH):
                    for k in range(zh):
                        mm = nc.tensor.matmul(m.psum[2 * i + 1][:, o, :], conv_w[:, k, o * P:(o + 1) * P],
                                              y[i][:, k, :], start=k == 0, stop=k == zh - 1)
                mm.then_inc(conv_done, 1)

            if w is not None:
                pe.wait_ge(w_in, 16 * kh)
            if layer == 0:
                for k in range(CH):
                    for c in range(CH):
                        mm = nc.tensor.matmul(m.psum[3][:, k, 0:C], w_view[:, c, k * P:(k + 1) * P],
                                              w_view[:, c, C:2 * C], start=c == 0, stop=c == CH - 1)
                mm.then_inc(merged, 1)
            pe.wait_ge(heads_copied, 1)
            pe.wait_ge(recip_in, 16)
            if layer == 0:
                pe.wait_ge(merge_copied, 1)
            blocks(pe, spread_recip, conv)

        @block.scalar
        def _(act):
            act.wait_ge(heads_in, 16)
            nc.scalar.activation(heads_of, heads_loaded, ACT.Copy).then_inc(heads_copied, 1)
            if layer == 0:
                act.wait_ge(merged, 1)
                nc.scalar.activation(conv_w, m.psum[3][:, :, 0:C], ACT.Copy).then_inc(merge_copied, 1)
                return

            def add_bias(p):
                for i in range(2):
                    n = p * 2 + i
                    act.wait_ge(divided, n + 1)
                    wait_count(act, x_done if layer == 1 else conv_done, n - 1)
                    col = {1: B_L1_V, 2: B_L2_V, 3: B_L3_V}[layer]
                    for k in range(zh):
                        op = nc.scalar.activation(y[i][:, k, :], z_in[i][:, k, :], ACT.Identity,
                                                  bias=m.bias[:, col + k:col + k + 1])
                    op.then_inc(y_ready, 1)

            passes(act, NB // 2, add_bias)

        @block.vector
        def _(dve):
            def divide(n, p, i):
                dve.wait_ge(spread, n + 1)
                dve.wait_ge(z_loaded[i], (p + 1) * (16 * zh))
                if layer == 0:
                    wait_count(dve, conv_done, n - 1)
                to = z_in[i] if layer else y[i]
                for k in range(zh):
                    op = nc.vector.tensor_tensor(to[:, k, :], z_in[i][:, k, :], m.psum[2 * i][:, k % rh, :], ALU.mult)
                op.then_inc(divided, 1)

            def add_x(n, i):
                dve.wait_ge(conv_done if layer != 1 else y_ready, n + 1)
                for k, xk in enumerate(x_of(n)):
                    if layer == 0:
                        op = nc.vector.tensor_tensor(xk, m.psum[2 * i + 1][:, k, :].rearrange("p (j c) -> p j c", j=2),
                                                     xk, ALU.add)
                    elif layer == 1:
                        op = nc.vector.scalar_tensor_tensor(out=xk, in0=y[i][:, k, :], scalar=m.bias[:, B_GAMMA:B_GAMMA + 1],
                                                            in1=xk, op0=ALU.mult, op1=ALU.add)
                    else:
                        col = {2: B_L2_O, 3: B_L3_O}[layer] + k
                        op = nc.vector.scalar_tensor_tensor(out=xk, in0=m.psum[2 * i + 1][:, k, :],
                                                            scalar=m.bias[:, col:col + 1], in1=xk,
                                                            op0=ALU.add, op1=ALU.add)
                op.then_inc(x_done, 1)

            dve.wait_ge(den_in, 16)
            nc.vector.reciprocal(packed, packed).then_inc(inverted, 1)
            dve.wait_ge(inverted, 1)
            nc.vector.tensor_copy(packed_parts[:, 0, :], packed).then_inc(inverted, 1)
            dve.wait_ge(inverted, 2)
            nc.vector.tensor_tensor(packed_parts[:, 1, :], packed, packed_parts[:, 0, :].bitcast(F32), ALU.subtract).then_inc(inverted, 1)
            blocks(dve, divide, add_x)


def build(nc, x, bias, const, proj0, proj1, proj2, proj3, fin0, fin2, fin3, out):
    with ExitStack() as ctx:
        m = Memory(nc, ctx)
        held = []

        def sem(name):
            held.append(nc.alloc_semaphore(name=name))
            return held[-1]

        load_phase(nc, sem, m, x, bias, const)
        for layer, (proj, fin) in enumerate(((proj0, fin0), (proj1, None), (proj2, fin2), (proj3, fin3))):
            project_phase(nc, sem, m, layer, proj)
            attention_phase(nc, sem, m, layer)
            finish_phase(nc, sem, m, layer, fin, const, out)
            nc.clear_and_free_semaphores(held)
            nc.all_engine_barrier()
            held.clear()


def _bias_table(np, i):
    table = np.zeros((P, B_COLS), np.float32)
    table[0:32, B_L1_QK] = i["L1_conv_bk"]
    table[32:64, B_L1_QK] = i["L1_conv_bq"]
    table[:, B_GAMMA] = i["L1_conv_gamma"][0]
    for col, name in ((B_L1_V, "L1_conv_bv"), (B_L2_Q, "L2_conv_bq"), (B_L2_K, "L2_conv_bk"), (B_L2_V, "L2_conv_bv"),
                      (B_L2_O, "L2_conv_bo"), (B_L3_O, "L3_conv_W_b")):
        table[:, col:col + 2] = i[name].reshape(2, P).T
    for col, name in ((B_L3_Q, "L3_conv_theta_b"), (B_L3_K, "L3_conv_phi_b"), (B_L3_V, "L3_conv_g_b")):
        table[:, col] = i[name]
    return table


def _const_table(np):
    eye = np.eye(P, dtype=np.float32)
    sum32 = np.tile(np.eye(32, dtype=np.float32), (4, 1))
    sum64 = np.tile(np.eye(64, dtype=np.float32), (2, 1))
    heads = [np.zeros((P, C), np.float32) for _ in K_HEADS]
    for table, H in zip(heads, K_HEADS):
        table[0:2 * H] = np.tile(np.repeat(np.eye(H, dtype=np.float32), C // H, axis=1), (2, 1))
    return np.concatenate([eye, np.ones((P, P), np.float32), sum32, sum64] + heads, axis=1)


def kernel(**inputs):
    import numpy as np
    import concourse.bacc as bacc
    from concourse.bass_utils import run_bass_kernel_spmd

    i = {k: np.asarray(v) for k, v in inputs.items()}

    def side_by_side(*names):
        return np.ascontiguousarray(np.concatenate([i[n].T for n in names], axis=1))

    arrays = {
        "x": np.ascontiguousarray(i["x"].reshape(C, T)),
        "bias": _bias_table(np, i),
        "const": _const_table(np),
        "proj0": side_by_side("L0_conv_Wf", "L0_conv_Wg", "L0_conv_Wh"),
        "proj1": side_by_side("L1_conv_wk", "L1_conv_wq", "L1_conv_wv"),
        "proj2": side_by_side("L2_conv_Wq", "L2_conv_Wk", "L2_conv_Wv"),
        "proj3": side_by_side("L3_conv_theta_w", "L3_conv_phi_w", "L3_conv_g_w"),
        "fin0": np.ascontiguousarray(np.concatenate([i["L0_conv_Wm"], i["L0_conv_Wv"].T], axis=1)),
        "fin2": side_by_side("L2_conv_Wo"),
        "fin3": side_by_side("L3_conv_W_w"),
    }
    nc = bacc.Bacc("TRN2", target_bir_lowering=False, num_devices=1)
    args = {n: nc.dram_tensor(f"in_{n}", a.shape, F32, kind="ExternalInput").ap() for n, a in arrays.items()}
    out = nc.dram_tensor("out_x", (C, T), F32, kind="ExternalOutput").ap()
    build(nc, out=out, **args)
    r = run_bass_kernel_spmd(nc, [{f"in_{n}": a for n, a in arrays.items()}], core_ids=[0])
    return r.results[0]["out_x"].reshape(1, C, 64, 64)
```
